# Optimizing a Trainium2 kernel written in Bass

```python
import numpy as np
import jax
import jax.numpy as jnp

def _softmax(x, axis=-1):
    return jax.nn.softmax(x, axis=axis)
def _gelu(x):
    return jax.nn.gelu(x, approximate=True)
def _silu(x):
    return jax.nn.silu(x)
def _sigmoid(x):
    return jax.nn.sigmoid(x)
def _layernorm(x, axis=-1, eps=1e-5):
    m = jnp.mean(x, axis=axis, keepdims=True)
    v = jnp.var(x, axis=axis, keepdims=True)
    return (x - m) / jnp.sqrt(v + eps)
def _scatter_add(tgt, idx, src, axis=0):
    return tgt.at[idx].add(src)
def _segment_sum(src, seg, n):
    return jax.ops.segment_sum(src, seg, n)

kernel_name = 'mk_conv_preact_d2_conv_nhwc16_09d8d3'

def setup_inputs(seed: int = 0):
    np.random.seed(seed)
    _w = jnp.asarray
    def _rec_inputs():
        import jax
        import jax.numpy as jnp
        _gk = jax.random.key(seed)
        x = -0.000125 + 0.9999 * jax.random.normal(jax.random.fold_in(_gk, 1), (8, 512, 512, 16), jnp.float32)
        return x
    x = _rec_inputs()
    def _L0_conv_setup():
        import jax, jax.numpy as jnp
        import numpy as np
        D_DIM, d_DIM, C_TUBE = (512, 512, 16)
        BATCH, N_COLS = (8, 512)

        def dct_matrix(c):
            k = np.arange(c)[:, None]
            n = np.arange(c)[None, :]
            M = np.sqrt(2.0 / c) * np.cos(np.pi * (2 * n + 1) * k / (2 * c))
            M[0, :] *= 1.0 / np.sqrt(2.0)
            return jnp.asarray(M, dtype=jnp.float32)
        key = jax.random.key(seed)
        k1, k2 = jax.random.split(key)
        x = jax.random.normal(k1, (BATCH, d_DIM, N_COLS, C_TUBE), dtype=jnp.float32)
        fan_in = d_DIM * C_TUBE
        bound = np.sqrt(6.0 / ((1.0 + 5.0) * fan_in))
        weight = jax.random.uniform(k2, (D_DIM, d_DIM, C_TUBE), dtype=jnp.float32, minval=-bound, maxval=bound)
        return {'x': x, 'weight': weight}
    _L0_conv_all = _L0_conv_setup()
    _L0_conv_in = {k: v for k, v in _L0_conv_all.items() if k in ('weight', )}
    del _L0_conv_all

    def _L1_conv_setup():
        import jax, jax.numpy as jnp
        import numpy as np
        key = jax.random.key(seed)
        k1, k2, k3 = jax.random.split(key, 3)
        x = jax.random.normal(k1, (16, 512, 512, 16), dtype=jnp.float32)
        filters = jax.random.normal(k2, (3, 3, 16, 16), dtype=jnp.float32) * 0.05
        bias = jax.random.normal(k3, (16,), dtype=jnp.float32) * 0.05
        return {'x': x, 'filters': filters, 'bias': bias}
    _L1_conv_all = _L1_conv_setup()
    _L1_conv_in = {k: v for k, v in _L1_conv_all.items() if k in ('filters', 'bias', )}
    del _L1_conv_all

    return {
        "x": x,
        "L0_conv_weight": _L0_conv_in["weight"],
        "L1_conv_filters": _L1_conv_in["filters"],
        "L1_conv_bias": _L1_conv_in["bias"],
    }

def reference(x, L0_conv_weight, L1_conv_filters, L1_conv_bias):
    import jax
    import jax.numpy as jnp
    def _L0_conv_ref(x, weight):
        import jax, jax.numpy as jnp
        import numpy as np
        D_DIM, d_DIM, C_TUBE = (512, 512, 16)
        BATCH, N_COLS = (8, 512)

        def dct_matrix(c):
            k = np.arange(c)[:, None]
            n = np.arange(c)[None, :]
            M = np.sqrt(2.0 / c) * np.cos(np.pi * (2 * n + 1) * k / (2 * c))
            M[0, :] *= 1.0 / np.sqrt(2.0)
            return jnp.asarray(M, dtype=jnp.float32)
        M = dct_matrix(C_TUBE)
        Ahat = jnp.einsum('Ddc,kc->Ddk', weight, M)
        Xhat = jnp.einsum('Ndnc,kc->Ndnk', x, M)
        Chat = jnp.einsum('Ddk,Ndnk->NDnk', Ahat, Xhat)
        out = jnp.einsum('NDnk,kc->NDnc', Chat, M)
        return out

    def _L1_conv_ref(x, filters, bias):
        import jax, jax.numpy as jnp
        import numpy as np
        out = jax.lax.conv_general_dilated(x, filters, window_strides=(1, 1), padding='SAME', dimension_numbers=('NHWC', 'HWIO', 'NHWC'))
        return out + bias

    def _gn(v, G=8, eps=1e-5):
        B_, H_, W_, C_ = v.shape
        g = v.reshape(B_, H_, W_, G, C_ // G)
        m = jnp.mean(g, axis=(1, 2, 4), keepdims=True)
        s = jnp.var(g, axis=(1, 2, 4), keepdims=True)
        return ((g - m) / jnp.sqrt(s + eps)).reshape(v.shape)

    def _ln_c(v, eps=1e-6):
        m = jnp.mean(v, axis=-1, keepdims=True)
        s = jnp.var(v, axis=-1, keepdims=True)
        return (v - m) / jnp.sqrt(s + eps)

    def _ln_t(v, eps=1e-5):
        m = jnp.mean(v, axis=-1, keepdims=True)
        s = jnp.var(v, axis=-1, keepdims=True)
        return (v - m) / jnp.sqrt(s + eps)

    def _to_tokens(v):
        B_, H_, W_, C_ = v.shape
        return v.reshape(B_, H_ * W_, C_)
    def _from_tokens(t, like):
        return t.reshape(like.shape)

    x = x + _L0_conv_ref(_gn(x), L0_conv_weight)
    x = x + _L1_conv_ref(_gn(x), L1_conv_filters, L1_conv_bias)
    return x


_drawn_inputs = setup_inputs


def setup_inputs(seed=0):
    import zlib

    import numpy as np

    out = dict(_drawn_inputs(seed))
    spreads = {}
    factors = {}
    for name, (base, spread) in spreads.items():
        noise = np.random.default_rng([zlib.crc32(name.encode()), seed]).standard_normal(out[name].shape)
        drawn = base * np.exp(spread * noise) if base else spread * noise
        out[name] = jnp.asarray(drawn.astype(out[name].dtype))
    for name, factor in factors.items():
        out[name] = (out[name] * factor).astype(out[name].dtype)
    return out
```

```python
import numpy as np
import concourse.bass as bass
from concourse import mybir
from contextlib import ExitStack

FP32 = mybir.dt.float32
FP16 = mybir.dt.float16
I32 = mybir.dt.int32
ALU = mybir.AluOpType
ACT = mybir.ActivationFunctionType
AX = mybir.AxisListType

B, H, W, C = 8, 512, 512, 16
P = 128
TW = P // C
NG = W // TW
NC_ = H // P
GROUPS, GC = 8, C // 8
EPS = 1e-5
GB = 4
NB = NG // GB
BW = GB * TW
BANK = 512
OW = TW + 2
NBANK = 8
STAGES = 4
HSLOTS = 12
XSCALE = 16.0
WTOP = 256.0
EXPONENT_BITS = 0x7F800000
LEAST = 1e-30

CONST_COLS = {}
_at = 0
for _name, _n in (("ident", P), ("dct", P), ("idct", P), ("mean_all", P), ("mean_group", P),
                  ("eighth", P), ("pick_group", GROUPS), ("pick_channel", C), ("centre", OW * C), ("ones", P)):
    CONST_COLS[_name] = (_at, _at + _n)
    _at += _n
CONST_N = _at


def shape_constants():
    k = np.arange(C)[:, None]
    n = np.arange(C)[None, :]
    m = np.sqrt(2.0 / C) * np.cos(np.pi * (2 * n + 1) * k / (2 * C))
    m[0, :] *= 1.0 / np.sqrt(2.0)
    p = np.arange(P)
    out = np.zeros((P, CONST_N), np.float32)

    def put(name, a):
        lo, hi = CONST_COLS[name]
        out[:, lo:hi] = a

    put("ident", np.eye(P))
    dct = np.zeros((TW, C, C, TW))
    for t in range(TW):
        dct[t, :, :, t] = m.T
    put("dct", dct.reshape(P, P))
    put("idct", dct.reshape(P, P).T)
    put("mean_all", np.full((P, P), 1.0 / P))
    same = ((p[:, None] % C) // GC == (p[None, :] % C) // GC)
    put("mean_group", same / (TW * GC))
    put("eighth", np.full((P, P), 1.0 / TW))
    put("pick_group", (p[:, None] % C) // GC == np.arange(GROUPS)[None, :])
    put("pick_channel", (p[:, None] % C) == np.arange(C)[None, :])
    centre = np.zeros((P, OW, C))
    centre[p, p // C + 1, p % C] = 1.0
    put("centre", centre.reshape(P, OW * C))
    put("ones", np.ones((P, P)))
    return out


class Tally:

    def __init__(self, sem):
        self.sem, self.n = sem, 0

    def done(self, instruction):
        self.n += 1
        instruction.then_inc(self.sem, 1)
        return self.n


def build(nc, x, weight, filters, bias, consts, out):
    ctx = ExitStack()
    with ctx:
        def sb(name, shape, dt=FP32):
            return ctx.enter_context(nc.sbuf_tensor(name, shape, dt))

        a_dram = nc.dram_tensor("a_split", (C, H, 2, H), FP16, kind="Internal").ap()

        Z = sb("image", [P, NG, BANK])
        Zx = Z[:, :, :].rearrange("p g (c w) -> p g c w", c=NC_)
        Z16 = Z[:, :, :].bitcast(FP16).rearrange("p g (c k s n) -> p g c k s n", c=NC_, k=C, s=2)
        Zw = Z[:, :, :].rearrange("p g w -> p (g w)").rearrange("p (o g w) -> p o g w", o=NC_, g=NG)
        arena = sb("arena", [P, HSLOTS * 2 * (H + 2)], FP16)
        a_ring = arena[:, 0:2 * NC_ * 2 * H].rearrange("p (r c s o) -> p r c s o", r=2, c=NC_, s=2)
        h_ring = arena[:, :].rearrange("p (r s h) -> p r s h", r=HSLOTS, s=2)
        stage = sb("stage", [P, 2, NC_, GB * P])
        out_stage = stage[:, :, :, :].rearrange("p a b w -> p (a b) w")
        a_stage = stage[:, 0, :, :].bitcast(FP16).rearrange("p r (s o) -> p r s o", s=2)
        xt = sb("transposed", [P, STAGES, BANK])
        con = sb("constants", [P, CONST_N])
        cst = {n: con[:, lo:hi] for n, (lo, hi) in CONST_COLS.items()}
        dct_r = sb("dct_scaled", [P, P])
        idct_s = sb("idct_scaled", [P, P])
        taps = sb("taps", [P, 3, OW * C])
        taps_s = sb("taps_scaled", [P, 3, OW * C])
        taps_hi = sb("taps_hi", [P, 3, OW * C], FP16)
        taps_lo = sb("taps_lo", [P, 3, OW * C], FP16)
        xstat = sb("x_stats", [P, GROUPS, NG // 8, 6])
        ystat = sb("y_stats", [P, NG, 6])
        small = sb("small", [P, 512])
        ps = ctx.enter_context(nc.psum_tensor("banks", [P, NBANK, BANK], FP32))

        def cols(n):
            at = small_at[0]
            small_at[0] += n
            return small[:, at:at + n]
        small_at = [0]

        a_scale, a_unscale = cols(1), cols(1)
        x_negmean, bias_p, tap_max = cols(1), cols(1), cols(1)
        h_scale, h_shift, conv_unscale = cols(1), cols(1), cols(1)
        out_shift = cols(C)
        mv8, mean8, dev8, t8a, t8b, var8, r8 = (cols(16) for _ in range(7))
        w_max = cols(8)
        c1 = [cols(1) for _ in range(16)]
        s16 = cols(16)
        row = cols(P)

        sems = []

        def sem(name):
            s = ctx.enter_context(nc.semaphore(name))
            sems.append(s)
            return s

        dve_step, pe_step, act_step = sem("dve_step"), sem("pe_step"), sem("act_step")
        const_in = sem("const_in")
        x_in = [sem(f"x_in{i}") for i in range(NB)]
        a_in = [sem(f"a_in{i}") for i in range(2)]
        restage_in = [sem(f"restage_in{i}") for i in range(2)]
        stored = [sem(f"stored{i}") for i in range(STAGES)]
        transposed = sem("transposed")
        xt_even, xt_odd = sem("xt_even"), sem("xt_odd")
        product = sem("product")
        hi_done, lo_done = sem("hi_done"), sem("lo_done")
        evac_a, evac_b = sem("evac_a"), sem("evac_b")
        h_done = sem("h_done")
        pads_zero = sem("pads_zero")
        nums = [s.num for s in sems]
        sem_range = range(min(nums), max(nums) + 1)
        assert len(sem_range) == len(sems)

        def end_phase():
            nc.all_engine_barrier(sems_to_clear=sem_range)


        def largest_everywhere(dve, t, pe_before):
            dve.wait_ge(pe_step, pe_before + 1)
            t.done(nc.vector.reduce_max(row[0:1, 0:1], ps[0:1, 0, 0:P], AX.X))
            dve.wait_ge(dve_step, t.n)
            t.done(nc.vector.tensor_scalar(row[0:1, 1:2], row[0:1, 0:1], LEAST, None, ALU.max))
            dve.wait_ge(pe_step, pe_before + 2)
            t.done(nc.vector.tensor_copy(c1[0], ps[:, 0, 256:257]))
            dve.wait_ge(dve_step, t.n)
            t.done(nc.vector.tensor_scalar(c1[1].bitcast(I32), c1[0].bitcast(I32), EXPONENT_BITS, None,
                                           ALU.bitwise_and))
            dve.wait_ge(dve_step, t.n)
            t.done(nc.vector.reciprocal(c1[2], c1[1]))
            dve.wait_ge(dve_step, t.n)

        def inverse_root(dve, t, var, r, ta, tb, root_in):
            t.done(nc.vector.reciprocal(r, root_in))
            dve.wait_ge(dve_step, t.n)
            t.done(nc.vector.tensor_tensor(ta, r, r, ALU.mult))
            dve.wait_ge(dve_step, t.n)
            t.done(nc.vector.tensor_tensor(tb, ta, var, ALU.mult))
            dve.wait_ge(dve_step, t.n)
            t.done(nc.vector.tensor_scalar(ta, tb, -0.5, 1.5, ALU.mult, ALU.add))
            dve.wait_ge(dve_step, t.n)
            t.done(nc.vector.tensor_tensor(r, r, ta, ALU.mult))
            dve.wait_ge(dve_step, t.n)

        def x_stats_of(dve, t, j):
            v = Z[:, 8 * j:8 * j + 8, :].rearrange("p g w -> p (g w)").rearrange("p (n c) -> p n c", c=C)
            for q in range(GROUPS):
                t.done(nc.vector.bn_stats(xstat[:, q, j, :], v[:, :, GC * q:GC * q + GC]))

        def x_final_dve(dve, t):
            dve.wait_ge(dve_step, t.n)
            mv = mv8.rearrange("p (q s) -> p q s", s=2)
            for q in range(GROUPS):
                t.done(nc.vector.bn_aggr(mv[:, q, :], xstat[:, q, :, :].rearrange("p j s -> p (j s)")))
            dve.wait_ge(dve_step, t.n)
            t.done(nc.vector.tensor_copy(t8a[:, 0:8], mv[:, :, 0]))
            base = t.n
            dve.wait_ge(pe_step, 1)
            t.done(nc.vector.tensor_copy(mean8[:, 0:8], ps[:, 0, 0:8]))
            dve.wait_ge(dve_step, t.n)
            t.done(nc.vector.tensor_tensor(dev8[:, 0:8], t8a[:, 0:8], mean8[:, 0:8], ALU.subtract))
            dve.wait_ge(dve_step, t.n)
            t.done(nc.vector.tensor_tensor(dev8[:, 8:16], dev8[:, 0:8], dev8[:, 0:8], ALU.mult))
            dve.wait_ge(dve_step, t.n)
            t.done(nc.vector.tensor_tensor(t8b[:, 0:8], dev8[:, 8:16], mv[:, :, 1], ALU.add))
            second = t.n
            dve.wait_ge(pe_step, 2)
            t.done(nc.vector.tensor_scalar(var8[:, 0:8], ps[:, 1, 0:8], EPS, None, ALU.add))
            third = t.n
            dve.wait_ge(act_step, 1)
            inverse_root(dve, t, var8[:, 0:8], r8[:, 0:8], t8a[:, 8:16], t8b[:, 8:16], var8[:, 8:16])
            t.done(nc.vector.tensor_tensor(s16[:, 0:8], r8[:, 0:8], cst["pick_group"], ALU.mult))
            t.done(nc.vector.tensor_tensor(s16[:, 8:16], mean8[:, 0:8], cst["pick_group"], ALU.mult))
            dve.wait_ge(dve_step, t.n)
            t.done(nc.vector.reduce_sum(c1[0], s16[:, 0:8], AX.X))
            t.done(nc.vector.reduce_sum(c1[1], s16[:, 8:16], AX.X))
            dve.wait_ge(dve_step, t.n)
            t.done(nc.vector.tensor_scalar(x_negmean, c1[1], -1.0, None, ALU.mult))
            t.done(nc.vector.tensor_scalar(dct_r[:, :], cst["dct"], c1[0], XSCALE, ALU.mult, ALU.mult))
            return base, second, third

        def x_final_pe(pe, base, second):
            pe.wait_ge(dve_step, base)
            nc.tensor.matmul(ps[:, 0, 0:8], cst["mean_all"], t8a[:, 0:8], start=True, stop=True).then_inc(pe_step, 1)
            pe.wait_ge(dve_step, second)
            nc.tensor.matmul(ps[:, 1, 0:8], cst["mean_all"], t8b[:, 0:8], start=True, stop=True).then_inc(pe_step, 1)

        def x_final_act(act, third):
            act.wait_ge(dve_step, third)
            nc.scalar.activation(var8[:, 8:16], var8[:, 0:8], ACT.Sqrt).then_inc(act_step, 1)

        def x_final_marks(n):
            return n + GROUPS + 1, n + GROUPS + 5, n + GROUPS + 6

        def load_x(eng, b, i):
            for c in range(NC_):
                src = x[b, c * P:(c + 1) * P, 2 * BW * i:2 * BW * (i + 1), :].rearrange("b p w k -> p (b w k)")
                eng.dma_start(Zx[:, 8 * i:8 * (i + 1), c, :], src.rearrange("p (g n) -> p g n", g=8))\
                   .then_inc(x_in[i], 16)

        X_LOADED = 16 * NC_


        with nc.Block() as block:
            @block.sync
            def _(sp):
                sp.dma_start(con[:, :], consts[:, :]).then_inc(const_in, 16)
                for o in range(NC_):
                    for h in range(2):
                        src = weight[o * P:(o + 1) * P, h * 256:(h + 1) * 256, :].rearrange("p d c -> p (d c)")
                        dst = Z[:, :, :].rearrange("p g w -> p (g w)")[:, (2 * o + h) * 4096:(2 * o + h + 1) * 4096]
                        sp.dma_start(dst, src).then_inc(x_in[2 * o + h], 16)
                sp.wait_ge(const_in, 16)

            @block.scalar
            def _(act):
                act.wait_ge(pads_zero, 1)
                for n in range(TW):
                    for dw in range(3):
                        at = (n - dw + 2) * C
                        act.dma_start(taps[n * C:(n + 1) * C, :, at:at + C],
                                      filters[:, dw, :, :].rearrange("h c o -> c h o")).then_inc(a_in[0], 16)
                    act.dma_start(bias_p[n * C:(n + 1) * C, :], bias.rearrange("(c a) -> c a", a=1)).then_inc(a_in[1], 16)
                act.wait_ge(a_in[0], 16 * 3 * TW)
                act.wait_ge(a_in[1], 16 * TW)

            @block.vector
            def _(dve):
                t = Tally(dve_step)
                nc.vector.memset(taps[:, :, :], 0.0).then_inc(pads_zero, 1)
                zf = Z[:, :, :].rearrange("p g w -> p (g w)")
                for i in range(8):
                    dve.wait_ge(x_in[i], 16)
                    t.done(nc.vector.tensor_reduce(w_max[:, i:i + 1], zf[:, i * 4096:(i + 1) * 4096], AX.X, ALU.max,
                                                   apply_absolute_value=True))
                dve.wait_ge(dve_step, t.n)
                t.done(nc.vector.reduce_max(c1[3], w_max, AX.X))
                assert t.n == 9
                largest_everywhere(dve, t, 0)
                t.done(nc.vector.tensor_scalar(a_scale, c1[2], WTOP, None, ALU.mult))
                t.done(nc.vector.tensor_scalar(a_unscale, c1[1], 1.0 / (WTOP * XSCALE), None, ALU.mult))
                dve.wait_ge(dve_step, t.n)
                t.done(nc.vector.tensor_scalar(idct_s[:, :], cst["idct"], a_unscale, None, ALU.mult))
                dve.wait_ge(a_in[0], 16 * 3 * TW)
                t.done(nc.vector.tensor_reduce(tap_max, taps[:, :, :].rearrange("p h w -> p (h w)"), AX.X, ALU.max,
                                               apply_absolute_value=True))

            @block.tensor
            def _(pe):
                pe.wait_ge(const_in, 16)
                pe.wait_ge(dve_step, 9)
                nc.tensor.transpose(ps[0:1, 0, 0:P], c1[3], cst["ident"]).then_inc(pe_step, 1)
                pe.wait_ge(dve_step, 11)
                nc.tensor.matmul(ps[:, 0, 256:257], cst["ones"][0:1, :], row[0:1, 1:2], start=True, stop=True).then_inc(pe_step, 1)
        end_phase()

        with nc.Block() as block:
            @block.sync
            def _(sp):
                for g in range(NG):
                    sp.wait_ge(lo_done, g + 1)
                    sp.dma_start(a_dram[:, TW * g:TW * (g + 1), :, :].rearrange("k n s o -> k n (s o)"),
                                 a_stage[:, g % STAGES, :, :].rearrange("p s o -> p (s o)"))\
                      .then_inc(stored[g % STAGES], 16)
                for r in range(STAGES):
                    sp.wait_ge(stored[r], 16 * (NG // STAGES))

            @block.tensor
            def _(pe):
                def transpose(g):
                    if g >= 2:
                        pe.wait_ge(xt_even, g - 1)
                    for o in range(NC_):
                        last = nc.tensor.transpose(ps[:, g % 2, o * P:(o + 1) * P], Zw[:, o, g, :], cst["ident"])
                    last.then_inc(transposed, 1)
                transpose(0)
                for g in range(NG):
                    if g + 1 < NG:
                        transpose(g + 1)
                    pe.wait_ge(xt_even, g + 1)
                    if g >= 4:
                        pe.wait_ge(lo_done, g - 3)
                    nc.tensor.matmul(ps[:, 2 + g % 4, :], cst["dct"], xt[:, g % STAGES, :], start=True, stop=True)\
                      .then_inc(product, 1)

            @block.scalar
            def _(act):
                for g in range(NG):
                    act.wait_ge(product, g + 1)
                    if g >= STAGES:
                        act.wait_ge(stored[g % STAGES], 16 * (g // STAGES))
                    nc.scalar.activation(a_stage[:, g % STAGES, 0, :], ps[:, 2 + g % 4, :], ACT.Copy, scale=a_scale)\
                      .then_inc(hi_done, 1)

            @block.vector
            def _(dve):
                def copy_out(g):
                    dve.wait_ge(transposed, g + 1)
                    if g >= STAGES:
                        dve.wait_ge(product, g - STAGES + 1)
                    nc.vector.tensor_copy(xt[:, g % STAGES, :], ps[:, g % 2, :]).then_inc(xt_even, 1)
                copy_out(0)
                for g in range(NG):
                    if g + 1 < NG:
                        copy_out(g + 1)
                    dve.wait_ge(hi_done, g + 1)
                    nc.vector.scalar_tensor_tensor(a_stage[:, g % STAGES, 1, :], ps[:, 2 + g % 4, :], a_scale,
                                                   a_stage[:, g % STAGES, 0, :], ALU.mult, ALU.subtract)\
                      .then_inc(lo_done, 1)
        end_phase()

        with nc.Block() as block:
            steps = GROUPS * (NG // 8)
            base, second, third = x_final_marks(steps)

            @block.sync
            def _(sp):
                for i in range(NG // 8):
                    load_x(sp, slice(0, 1), i)

            @block.vector
            def _(dve):
                t = Tally(dve_step)
                for j in range(NG // 8):
                    dve.wait_ge(x_in[j], X_LOADED)
                    x_stats_of(dve, t, j)
                assert x_final_dve(dve, t) == (base, second, third)

            @block.tensor
            def _(pe):
                x_final_pe(pe, base, second)

            @block.scalar
            def _(act):
                x_final_act(act, third)
        end_phase()


        def load_a(sp, k):
            sp.dma_start(a_ring[:, k % 2, :, :, :], a_dram[k, :, :, :].rearrange("(c p) s o -> p c s o", p=P))\
              .then_inc(a_in[k % 2], 16)

        def transform():
            with nc.Block() as block:
                @block.sync
                def _(sp):
                    for k in range(2):
                        load_a(sp, k)
                    for k in range(2):
                        sp.wait_ge(a_in[k], 16)

                @block.tensor
                def _(pe):
                    def transpose(g):
                        if g >= 2:
                            pe.wait_ge(xt_odd if g % 2 else xt_even, g // 2)
                        for c in range(NC_):
                            last = nc.tensor.transpose(ps[:, g % 2, c * P:(c + 1) * P], Zx[:, g, c, :], cst["ident"])
                        last.then_inc(transposed, 1)
                    transpose(0)
                    for g in range(NG):
                        if g + 1 < NG:
                            transpose(g + 1)
                        pe.wait_ge(xt_odd if g % 2 else xt_even, g // 2 + 1)
                        if g >= 4:
                            pe.wait_ge(lo_done, g - 3)
                        for c in range(NC_):
                            last = nc.tensor.matmul(ps[:, 2 + g % 4, c * P:(c + 1) * P],
                                                    xt[:, g % STAGES, c * P:(c + 1) * P], dct_r[:, :],
                                                    start=True, stop=True)
                        last.then_inc(product, 1)

                def bank(g):
                    return ps[:, 2 + g % 4, :].rearrange("p (c k n) -> p (c k) n", c=NC_, k=C)

                def part(g, s):
                    return Z16[:, g, :, :, s, :].rearrange("p c k n -> p (c k) n")

                def wait_centre(eng, g):
                    eng.wait_ge(transposed, g + 1)
                    if g >= STAGES:
                        eng.wait_ge(product, g - STAGES + 1)

                @block.scalar
                def _(act):
                    def centre(g):
                        wait_centre(act, g)
                        nc.scalar.activation(xt[:, g % STAGES, :], ps[:, g % 2, :], ACT.Identity, bias=x_negmean)\
                          .then_inc(xt_even, 1)
                    centre(0)
                    for g in range(NG):
                        if g % 2 and g + 1 < NG:
                            centre(g + 1)
                        act.wait_ge(product, g + 1)
                        nc.scalar.activation(part(g, 0), bank(g), ACT.Copy).then_inc(hi_done, 1)

                @block.vector
                def _(dve):
                    for g in range(NG):
                        if g % 2 == 0:
                            wait_centre(dve, g + 1)
                            nc.vector.tensor_scalar(xt[:, (g + 1) % STAGES, :], ps[:, (g + 1) % 2, :], x_negmean, None,
                                                    ALU.add).then_inc(xt_odd, 1)
                        dve.wait_ge(hi_done, g + 1)
                        nc.vector.tensor_tensor(part(g, 1), bank(g), part(g, 0), ALU.subtract).then_inc(lo_done, 1)
            end_phase()

        def restage(sp, b, j):
            src = x[b, :, BW * j:BW * (j + 1), :].rearrange("b (c p) w k -> p (b c) (w k)", p=P)
            sp.dma_start(stage[:, j % 2, :, :], src).then_inc(restage_in[j % 2], 16)

        def mix(b):
            with nc.Block() as block:
                @block.sync
                def _(sp):
                    for j in range(2):
                        restage(sp, b, j)
                    for k in range(2, C):
                        sp.wait_ge(product, k - 1)
                        load_a(sp, k)
                    for j in range(2):
                        sp.wait_ge(restage_in[j], 16)

                @block.tensor
                def _(pe):
                    for k in range(C):
                        if k >= 2:
                            pe.wait_ge(a_in[k % 2], 16 * (k // 2))
                            pe.wait_ge(evac_a, k - 1)
                            pe.wait_ge(evac_b, k - 1)
                        for o in range(NC_):
                            bank = ps[:, NC_ * (k % 2) + o, :].rearrange("p (g n) -> p g n", n=TW)
                            for c in range(NC_):
                                for w_part, x_part in ((0, 0), (0, 1), (1, 0)):
                                    last = nc.tensor.matmul(bank, a_ring[:, k % 2, c, w_part, o * P:(o + 1) * P],
                                                            Z16[:, :, c, k, x_part, :],
                                                            start=(c == 0 and w_part == 0 and x_part == 0),
                                                            stop=(c == NC_ - 1 and w_part == 1))
                        last.then_inc(product, 1)

                def view(k, half):
                    o = 2 * half
                    src = ps[:, NC_ * (k % 2) + o:NC_ * (k % 2) + o + 2, :].rearrange("p o (g n) -> p o g n", n=TW)
                    z = Z[:, :, :].rearrange("p g (o k n) -> p o g k n", o=NC_, k=C)
                    return z[:, o:o + 2, :, k, :], src

                @block.scalar
                def _(act):
                    for k in range(C):
                        act.wait_ge(product, k + 1)
                        dst, src = view(k, 0)
                        nc.scalar.activation(dst, src, ACT.Copy).then_inc(evac_a, 1)

                @block.vector
                def _(dve):
                    for k in range(C):
                        dve.wait_ge(product, k + 1)
                        dst, src = view(k, 1)
                        nc.vector.tensor_copy(dst, src).then_inc(evac_b, 1)
            end_phase()

        def y_final(dve, t):
            mean_p, var_p = mv8[:, 0:1], mv8[:, 1:2]
            dve.wait_ge(dve_step, t.n)
            t.done(nc.vector.bn_aggr(mv8[:, 0:2], ystat[:, :, :].rearrange("p g s -> p (g s)")))
            yield "mean"
            dve.wait_ge(pe_step, 1)
            t.done(nc.vector.tensor_copy(c1[4], ps[:, 0, 0:1]))
            dve.wait_ge(dve_step, t.n)
            t.done(nc.vector.tensor_tensor(c1[5], mean_p, c1[4], ALU.subtract))
            dve.wait_ge(dve_step, t.n)
            t.done(nc.vector.tensor_tensor(c1[6], c1[5], c1[5], ALU.mult))
            dve.wait_ge(dve_step, t.n)
            t.done(nc.vector.tensor_tensor(c1[7], c1[6], var_p, ALU.add))
            yield "moment"
            dve.wait_ge(pe_step, 2)
            t.done(nc.vector.tensor_scalar(c1[8], ps[:, 1, 0:1], EPS, None, ALU.add))
            yield "variance"
            dve.wait_ge(act_step, 1)
            inverse_root(dve, t, c1[8], c1[9], c1[10], c1[11], c1[12])
            t.done(nc.vector.tensor_tensor(c1[13], c1[8], c1[9], ALU.mult))
            t.done(nc.vector.tensor_scalar(h_scale, c1[9], XSCALE, None, ALU.mult))
            t.done(nc.vector.tensor_tensor(c1[14], c1[4], bias_p, ALU.add))
            dve.wait_ge(dve_step, t.n)
            t.done(nc.vector.tensor_tensor(c1[3], c1[13], tap_max, ALU.max))
            t.done(nc.vector.tensor_scalar(h_shift, c1[4], h_scale, -1.0, ALU.mult, ALU.mult))
            t.done(nc.vector.tensor_scalar(s16, cst["pick_channel"], c1[14], None, ALU.mult))
            t.done(nc.vector.scalar_tensor_tensor(taps_s[:, 1, :], cst["centre"], c1[13], taps[:, 1, :],
                                                  ALU.mult, ALU.add))
            yield "largest"
            largest_everywhere(dve, t, 2)
            t.done(nc.vector.tensor_scalar(c1[15], c1[2], WTOP, None, ALU.mult))
            t.done(nc.vector.tensor_scalar(conv_unscale, c1[1], 1.0 / (WTOP * XSCALE), None, ALU.mult))
            dve.wait_ge(dve_step, t.n)
            for h in (0, 2):
                t.done(nc.vector.tensor_scalar(taps_s[:, h, :], taps[:, h, :], c1[15], None, ALU.mult))
            t.done(nc.vector.tensor_scalar(taps_s[:, 1, :], taps_s[:, 1, :], c1[15], None, ALU.mult))
            dve.wait_ge(dve_step, t.n)
            t.done(nc.vector.tensor_copy(taps_hi[:, :, :], taps_s[:, :, :]))
            dve.wait_ge(dve_step, t.n)
            t.done(nc.vector.tensor_tensor(taps_lo[:, :, :], taps_s[:, :, :], taps_hi[:, :, :], ALU.subtract))
            dve.wait_ge(pe_step, 5)
            t.done(nc.vector.tensor_copy(out_shift, ps[:, 1, 256:256 + C]))

        Y_MARKS = {"mean": 1, "moment": 5, "variance": 6, "largest": 6 + 5 + 7}

        def back(b):
            with nc.Block() as block:
                @block.sync
                def _(sp):
                    for j in range(2, NB):
                        sp.wait_ge(product, GB * (j - 1))
                        restage(sp, b, j)

                @block.tensor
                def _(pe):
                    def transpose(g):
                        if g >= 2:
                            pe.wait_ge(xt_even, g - 1)
                        for o in range(NC_):
                            last = nc.tensor.transpose(ps[:, g % 2, o * P:(o + 1) * P], Zx[:, g, o, :], cst["ident"])
                        last.then_inc(transposed, 1)
                    transpose(0)
                    for g in range(NG):
                        if g + 1 < NG:
                            transpose(g + 1)
                        j, i = divmod(g, GB)
                        pe.wait_ge(xt_even, g + 1)
                        if g >= 4:
                            pe.wait_ge(evac_a, g - 3)
                        nc.tensor.matmul(ps[:, 2 + g % 4, :], idct_s[:, :], xt[:, g % STAGES, :], start=True, stop=False,
                                         skip_group_check=True)
                        if j >= 2:
                            pe.wait_ge(restage_in[j % 2], 16 * (j // 2))
                        for c in range(NC_):
                            last = nc.tensor.matmul(ps[:, 2 + g % 4, c * P:(c + 1) * P],
                                                    stage[:, j % 2, c, i * P:(i + 1) * P], cst["ident"],
                                                    start=False, stop=(c == NC_ - 1), is_transpose=True,
                                                    skip_group_check=True)
                        last.then_inc(product, 1)
                    pe.wait_ge(dve_step, NG + Y_MARKS["mean"])
                    nc.tensor.matmul(ps[:, 0, 0:1], cst["mean_group"], mv8[:, 0:1], start=True, stop=True).then_inc(pe_step, 1)
                    pe.wait_ge(dve_step, NG + Y_MARKS["moment"])
                    nc.tensor.matmul(ps[:, 1, 0:1], cst["mean_group"], c1[7], start=True, stop=True).then_inc(pe_step, 1)
                    pe.wait_ge(dve_step, NG + Y_MARKS["largest"])
                    nc.tensor.transpose(ps[0:1, 0, 0:P], c1[3], cst["ident"]).then_inc(pe_step, 1)
                    pe.wait_ge(dve_step, NG + Y_MARKS["largest"] + 2)
                    nc.tensor.matmul(ps[:, 0, 256:257], cst["ones"][0:1, :], row[0:1, 1:2], start=True, stop=True).then_inc(pe_step, 1)
                    nc.tensor.matmul(ps[:, 1, 256:256 + C], cst["eighth"], s16, start=True, stop=True).then_inc(pe_step, 1)

                @block.scalar
                def _(act):
                    for g in range(NG):
                        act.wait_ge(product, g + 1)
                        nc.scalar.activation(Z[:, g, :], ps[:, 2 + g % 4, :], ACT.Copy).then_inc(evac_a, 1)
                    act.wait_ge(dve_step, NG + Y_MARKS["variance"])
                    nc.scalar.activation(c1[12], c1[8], ACT.Sqrt).then_inc(act_step, 1)

                @block.vector
                def _(dve):
                    t = Tally(dve_step)

                    def copy_out(g):
                        dve.wait_ge(transposed, g + 1)
                        if g >= STAGES:
                            dve.wait_ge(product, g - STAGES + 1)
                        nc.vector.tensor_copy(xt[:, g % STAGES, :], ps[:, g % 2, :]).then_inc(xt_even, 1)

                    def stats(g):
                        dve.wait_ge(evac_a, g + 1)
                        t.done(nc.vector.bn_stats(ystat[:, g, :], Z[:, g, :]))
                    copy_out(0)
                    for g in range(NG):
                        if g + 1 < NG:
                            copy_out(g + 1)
                        if g >= 1:
                            stats(g - 1)
                    stats(NG - 1)
                    for mark in y_final(dve, t):
                        assert t.n == NG + Y_MARKS[mark], (mark, t.n - NG)
            end_phase()

        def convolve(b, following):
            with nc.Block() as block:
                @block.sync
                def _(sp):
                    for j in range(NB):
                        if following is not None and j % 2:
                            sp.wait_ge(lo_done, GB * (j + 1))
                            load_x(sp, following, j // 2)
                        for c in range(NC_):
                            n = NC_ * j + c
                            sp.wait_ge(evac_b, n + 1)
                            dst = out[b, c * P:(c + 1) * P, BW * j:BW * (j + 1), :].rearrange("b p w k -> p (b w k)")
                            sp.dma_start(dst, out_stage[:, n % STAGES, :]).then_inc(stored[n % STAGES], 16)
                    for r in range(STAGES):
                        sp.wait_ge(stored[r], 16 * (NB * NC_ // STAGES))

                @block.tensor
                def _(pe):
                    pe.wait_ge(pads_zero, 2)
                    for j in range(NB):
                        pe.wait_ge(lo_done, min(GB * (j + 1) + 1, NG))
                        pieces = [(GB * j + i, (TW * i - 1) * C, 0, OW * C) for i in range(GB)]
                        pieces[0] = (GB * j, 0, C, OW * C)
                        pieces[-1] = (GB * j + GB - 1, (TW * (GB - 1) - 1) * C, 0, (OW - 1) * C)
                        if j > 0:
                            pieces.append((GB * j - 1, 0, (OW - 1) * C, OW * C))
                        if j < NB - 1:
                            pieces.append((GB * (j + 1), (BW - 1) * C, 0, C))
                        for c in range(NC_):
                            n = NC_ * j + c
                            if n >= NBANK:
                                pe.wait_ge(evac_b, n - NBANK + 1)
                            for i, (g, at, lo, hi) in enumerate(pieces):
                                for dh in range(3):
                                    for s, t_part in ((0, taps_hi), (0, taps_lo), (1, taps_hi)):
                                        last = nc.tensor.matmul(
                                            ps[:, n % NBANK, at:at + hi - lo],
                                            h_ring[:, g % HSLOTS, s, c * P + dh:c * P + dh + P], t_part[:, dh, lo:hi],
                                            start=(i == 0 and dh == 0 and s == 0 and t_part is taps_hi),
                                            stop=(i == len(pieces) - 1 and dh == 2 and s == 1),
                                            skip_group_check=True)
                            last.then_inc(product, 1)
                    if following is not None:
                        pe.wait_ge(evac_b, NB * NC_)
                        x_final_pe(pe, base, second)

                @block.scalar
                def _(act):
                    for g in range(NG):
                        act.wait_ge(h_done, g + 1)
                        if g >= HSLOTS:
                            act.wait_ge(product, NC_ * ((g - HSLOTS + 1) // GB + 1))
                        nc.scalar.activation(h_ring[:, g % HSLOTS, 0, 1:H + 1], Z[:, g, :], ACT.Copy).then_inc(hi_done, 1)
                    if following is not None:
                        x_final_act(act, third)

                @block.vector
                def _(dve):
                    t = Tally(dve_step)
                    for edge in (0, H + 1):
                        nc.vector.memset(h_ring[:, :, :, edge:edge + 1], 0.0).then_inc(pads_zero, 1)

                    def normalize(g):
                        nc.vector.tensor_scalar(Z[:, g, :], Z[:, g, :], h_scale, h_shift, ALU.mult, ALU.add)\
                          .then_inc(h_done, 1)

                    def low_part(g):
                        dve.wait_ge(hi_done, g + 1)
                        nc.vector.tensor_tensor(h_ring[:, g % HSLOTS, 1, 1:H + 1], Z[:, g, :],
                                                h_ring[:, g % HSLOTS, 0, 1:H + 1], ALU.subtract).then_inc(lo_done, 1)

                    done = [0]

                    def split_to(upto):
                        while done[0] < upto:
                            g = done[0]
                            if g == 0:
                                normalize(0)
                            if g + 1 < NG:
                                normalize(g + 1)
                            low_part(g)
                            done[0] += 1

                    shift = out_shift.rearrange("p (a c) -> p a c", a=1).to_broadcast([P, BW, C])
                    split_to(GB + 1)
                    for j in range(NB):
                        split_to(min(GB * (j + 2) + 1, NG))
                        if following is not None and j % 2 and j >= 3:
                            i = (j - 3) // 2
                            dve.wait_ge(x_in[i], X_LOADED)
                            x_stats_of(dve, t, i)
                        for c in range(NC_):
                            n = NC_ * j + c
                            dve.wait_ge(product, n + 1)
                            if n >= STAGES:
                                dve.wait_ge(stored[n % STAGES], 16 * (n // STAGES))
                            nc.vector.scalar_tensor_tensor(
                                out_stage[:, n % STAGES, :].rearrange("p (w k) -> p w k", k=C),
                                ps[:, n % NBANK, :].rearrange("p (w k) -> p w k", k=C), conv_unscale, shift,
                                ALU.mult, ALU.add).then_inc(evac_b, 1)
                    if following is not None:
                        i = NG // 8 - 1
                        dve.wait_ge(x_in[i], X_LOADED)
                        x_stats_of(dve, t, i)
                        assert x_final_dve(dve, t) == (base, second, third)
            end_phase()

        with nc.Fori(0, B - 1) as b:
            here = bass.ds(b, 1)
            transform()
            mix(here)
            back(here)
            convolve(here, bass.ds(b + 1, 1))
        here = slice(B - 1, B)
        transform()
        mix(here)
        back(here)
        convolve(here, None)


_INS = ["x", "L0_conv_weight", "L1_conv_filters", "L1_conv_bias"]


def kernel(**inputs):
    import concourse.bacc as _bacc
    from concourse.bass_utils import run_bass_kernel_spmd as _run

    nc = _bacc.Bacc("TRN2", target_bir_lowering=False, num_devices=1)
    arrays, args = {}, []
    for name in _INS + ["consts"]:
        a = shape_constants() if name == "consts" else np.ascontiguousarray(inputs[name])
        arrays[f"in_{name}"] = a
        args.append(nc.dram_tensor(f"in_{name}", a.shape, FP32, kind="ExternalInput").ap())
    out = nc.dram_tensor("out", (B, H, W, C), FP32, kind="ExternalOutput").ap()
    build(nc, *args, out)
    r = _run(nc, [arrays], core_ids=[0])
    return r.results[0]["out"]
```

```python
import numpy as np
import concourse.bass as bass
from concourse import mybir
from contextlib import ExitStack

FP32 = mybir.dt.float32
FP16 = mybir.dt.float16
I32 = mybir.dt.int32
ALU = mybir.AluOpType
ACT = mybir.ActivationFunctionType
AX = mybir.AxisListType

B, H, W, C = 8, 512, 512, 16
P = 128
TW = P // C
NG = W // TW
NC_ = H // P
GROUPS, GC = 8, C // 8
EPS = 1e-5
GB = 4
NB = NG // GB
BW = GB * TW
BANK = 512
OW = TW + 2
AHEAD = 4
CBANKS = 7
SMALL = 7
STAGES = 4
REGION_LAG = TW // 2
HSLOTS = 12
XSCALE = 16.0
WTOP = 256.0
EXPONENT_BITS = 0x7F800000
LEAST = 1e-30

CONST_COLS = {}
_at = 0
for _name, _n in (("ident", P), ("dct", P), ("idct", P), ("mean_all", P), ("mean_group", P),
                  ("eighth", P), ("pick_group", GROUPS), ("pick_channel", C), ("centre", OW * C), ("ones", P)):
    CONST_COLS[_name] = (_at, _at + _n)
    _at += _n
CONST_N = _at


def shape_constants():
    k = np.arange(C)[:, None]
    n = np.arange(C)[None, :]
    m = np.sqrt(2.0 / C) * np.cos(np.pi * (2 * n + 1) * k / (2 * C))
    m[0, :] *= 1.0 / np.sqrt(2.0)
    p = np.arange(P)
    out = np.zeros((P, CONST_N), np.float32)

    def put(name, a):
        lo, hi = CONST_COLS[name]
        out[:, lo:hi] = a

    put("ident", np.eye(P))
    dct = np.zeros((TW, C, C, TW))
    for t in range(TW):
        dct[t, :, :, t] = m.T
    put("dct", dct.reshape(P, P))
    put("idct", dct.reshape(P, P).T)
    put("mean_all", np.full((P, P), 1.0 / P))
    same = ((p[:, None] % C) // GC == (p[None, :] % C) // GC)
    put("mean_group", same / (TW * GC))
    put("eighth", np.full((P, P), 1.0 / TW))
    put("pick_group", (p[:, None] % C) // GC == np.arange(GROUPS)[None, :])
    put("pick_channel", (p[:, None] % C) == np.arange(C)[None, :])
    centre = np.zeros((P, OW, C))
    centre[p, p // C + 1, p % C] = 1.0
    put("centre", centre.reshape(P, OW * C))
    put("ones", np.ones((P, P)))
    return out


class Tally:

    def __init__(self, sem):
        self.sem, self.n = sem, 0

    def done(self, instruction):
        self.n += 1
        instruction.then_inc(self.sem, 1)
        return self.n


def build(nc, x, weight, filters, bias, consts, out):
    ctx = ExitStack()
    with ctx:
        def sb(name, shape, dt=FP32):
            return ctx.enter_context(nc.sbuf_tensor(name, shape, dt))

        a_dram = nc.dram_tensor("a_split", (C, H, 2, H), FP16, kind="Internal").ap()

        Z = sb("image", [P, NG, BANK])
        Zx = Z[:, :, :].rearrange("p g (c w) -> p g c w", c=NC_)
        Z16 = Z[:, :, :].bitcast(FP16).rearrange("p g (c k s n) -> p g c k s n", c=NC_, k=C, s=2)
        arena = sb("arena", [P, HSLOTS * 2 * (H + 2)], FP16)
        a_ring = arena[:, 0:2 * NC_ * 2 * H].rearrange("p (r c s o) -> p r c s o", r=2, c=NC_, s=2)
        h_ring = arena[:, :].rearrange("p (r s h) -> p r s h", r=HSLOTS, s=2)
        stage = sb("stage", [P, 2, NC_, GB * P])
        out_stage = stage[:, :, :, :].rearrange("p a b w -> p (a b) w")
        a_stage = stage[:, 0, :, :].bitcast(FP16).rearrange("p r (s o) -> p r s o", s=2)
        xt = sb("transposed", [P, STAGES, BANK])
        con = sb("constants", [P, CONST_N])
        cst = {n: con[:, lo:hi] for n, (lo, hi) in CONST_COLS.items()}
        dct_r = sb("dct_scaled", [P, P])
        idct_s = sb("idct_scaled", [P, P])
        taps = sb("taps", [P, 3, OW * C])
        taps_s = sb("taps_scaled", [P, 3, OW * C])
        taps_hi = sb("taps_hi", [P, 3, OW * C], FP16)
        taps_lo = sb("taps_lo", [P, 3, OW * C], FP16)
        xstat = sb("x_stats", [P, GROUPS, NG // 8, 6])
        ystat = sb("y_stats", [P, NG, 6])
        small = sb("small", [P, 512])
        ps = ctx.enter_context(nc.psum_tensor("banks", [P, SMALL + 1, BANK], FP32))

        def cols(n):
            at = small_at[0]
            small_at[0] += n
            return small[:, at:at + n]
        small_at = [0]

        a_scale, a_unscale = cols(1), cols(1)
        x_negmean, bias_p, tap_max = cols(1), cols(1), cols(1)
        h_scale, h_shift, conv_unscale = cols(1), cols(1), cols(1)
        out_shift = cols(C)
        mv8, mean8, dev8, t8a, t8b, var8, r8 = (cols(16) for _ in range(7))
        w_max = cols(8)
        c1 = [cols(1) for _ in range(16)]
        s16, x_pick, x_own = cols(16), cols(16), cols(2)
        row = cols(P)

        sems = []

        def sem(name):
            s = ctx.enter_context(nc.semaphore(name))
            sems.append(s)
            return s

        const_in, taps_in, bias_in, taps_zero = sem("const_in"), sem("taps_in"), sem("bias_in"), sem("taps_zero")
        x_in = [sem(f"x_in{i}") for i in range(NG // 8)]
        w_in = [sem(f"w_in{i}") for i in range(NG // 8)]
        a_in = [sem(f"a_in{i}") for i in range(2)]
        restage_in = [sem(f"restage_in{i}") for i in range(2)]
        stored = [sem(f"stored{i}") for i in range(STAGES)]
        f_transposed, f_even, f_odd = sem("f_transposed"), sem("f_even"), sem("f_odd")
        f_product, f_hi, f_lo = sem("f_product"), sem("f_hi"), sem("f_lo")
        m_product, m_act, m_dve = sem("m_product"), sem("m_act"), sem("m_dve")
        b_transposed, b_even, b_odd = sem("b_transposed"), sem("b_even"), sem("b_odd")
        b_product, b_kept = sem("b_product"), sem("b_kept")
        pads_zero = sem("pads_zero")
        c_hi, c_norm, c_lo, c_product, c_out = (sem(n) for n in ("c_hi", "c_norm", "c_lo", "c_product", "c_out"))
        x_dve, x_pe, x_act = sem("x_dve"), sem("x_pe"), sem("x_act")
        y_dve, y_pe, y_act = sem("y_dve"), sem("y_pe"), sem("y_act")
        nums = [s.num for s in sems]
        sem_range = range(min(nums), max(nums) + 1)
        assert len(sem_range) == len(sems)

        def end_block():
            nc.all_engine_barrier(sems_to_clear=sem_range)


        def largest_everywhere(dve, t, pe_sem, pe_before):
            dve.wait_ge(pe_sem, pe_before + 1)
            t.done(nc.vector.reduce_max(row[0:1, 0:1], ps[0:1, SMALL, 0:P], AX.X))
            dve.wait_ge(t.sem, t.n)
            t.done(nc.vector.tensor_scalar(row[0:1, 1:2], row[0:1, 0:1], LEAST, None, ALU.max))
            dve.wait_ge(pe_sem, pe_before + 2)
            t.done(nc.vector.tensor_scalar(c1[1].bitcast(I32), ps[:, SMALL, 256:257].bitcast(I32), EXPONENT_BITS,
                                           None, ALU.bitwise_and))
            dve.wait_ge(t.sem, t.n)
            t.done(nc.vector.reciprocal(c1[2], c1[1]))
            dve.wait_ge(t.sem, t.n)

        def largest_transpose(pe_sem):
            nc.tensor.transpose(ps[0:1, SMALL, 0:P], c1[3], cst["ident"]).then_inc(pe_sem, 1)

        def largest_broadcast(pe_sem):
            nc.tensor.matmul(ps[:, SMALL, 256:257], cst["ones"][0:1, :], row[0:1, 1:2], start=True, stop=True)\
              .then_inc(pe_sem, 1)

        def inverse_root(dve, t, var, r, ta, tb, root):
            t.done(nc.vector.reciprocal(r, root))
            dve.wait_ge(t.sem, t.n)
            t.done(nc.vector.tensor_tensor(ta, r, r, ALU.mult))
            dve.wait_ge(t.sem, t.n)
            t.done(nc.vector.tensor_tensor(tb, ta, var, ALU.mult))
            dve.wait_ge(t.sem, t.n)
            t.done(nc.vector.tensor_scalar(ta, tb, -0.5, 1.5, ALU.mult, ALU.add))
            dve.wait_ge(t.sem, t.n)
            t.done(nc.vector.tensor_tensor(r, r, ta, ALU.mult))
            dve.wait_ge(t.sem, t.n)

        def x_stats_of(dve, t, i):
            dve.wait_ge(x_in[i], X_LOADED)
            v = Z[:, 8 * i:8 * i + 8, :].rearrange("p g w -> p (g w)").rearrange("p (n c) -> p n c", c=C)
            for q in range(GROUPS):
                t.done(nc.vector.bn_stats(xstat[:, q, i, :], v[:, :, GC * q:GC * q + GC]))

        x_mv = mv8.rearrange("p (q s) -> p q s", s=2)
        X_MEANS = GROUPS * (NG // 8) + GROUPS + 1
        X_MOMENTS, X_VARIANCES = X_MEANS + 4, X_MEANS + 5

        def x_means(dve, t):
            dve.wait_ge(t.sem, t.n)
            for q in range(GROUPS):
                t.done(nc.vector.bn_aggr(x_mv[:, q, :], xstat[:, q, :, :].rearrange("p j s -> p (j s)")))
            dve.wait_ge(t.sem, t.n)
            t.done(nc.vector.tensor_copy(t8a[:, 0:8], x_mv[:, :, 0]))
            assert t.n == X_MEANS

        def x_moments(dve, t):
            dve.wait_ge(x_pe, 1)
            t.done(nc.vector.tensor_copy(mean8[:, 0:8], ps[:, SMALL, 0:8]))
            dve.wait_ge(t.sem, t.n)
            t.done(nc.vector.tensor_tensor(dev8[:, 0:8], t8a[:, 0:8], mean8[:, 0:8], ALU.subtract))
            dve.wait_ge(t.sem, t.n)
            t.done(nc.vector.tensor_tensor(dev8[:, 8:16], dev8[:, 0:8], dev8[:, 0:8], ALU.mult))
            dve.wait_ge(t.sem, t.n)
            t.done(nc.vector.tensor_tensor(t8b[:, 0:8], dev8[:, 8:16], x_mv[:, :, 1], ALU.add))
            assert t.n == X_MOMENTS

        def x_scales(dve, t):
            dve.wait_ge(x_pe, 2)
            t.done(nc.vector.tensor_scalar(var8[:, 0:8], ps[:, SMALL, 8:16], EPS, None, ALU.add))
            assert t.n == X_VARIANCES
            dve.wait_ge(x_act, 1)
            inverse_root(dve, t, var8[:, 0:8], r8[:, 0:8], t8a[:, 8:16], t8b[:, 8:16], var8[:, 8:16])
            t.done(nc.vector.tensor_tensor(x_pick[:, 0:8], r8[:, 0:8], cst["pick_group"], ALU.mult))
            t.done(nc.vector.tensor_tensor(x_pick[:, 8:16], mean8[:, 0:8], cst["pick_group"], ALU.mult))
            dve.wait_ge(t.sem, t.n)
            t.done(nc.vector.reduce_sum(x_own[:, 0:1], x_pick[:, 0:8], AX.X))
            t.done(nc.vector.reduce_sum(x_own[:, 1:2], x_pick[:, 8:16], AX.X))
            dve.wait_ge(t.sem, t.n)
            t.done(nc.vector.tensor_scalar(x_negmean, x_own[:, 1:2], -1.0, None, ALU.mult))
            t.done(nc.vector.tensor_scalar(dct_r[:, :], cst["dct"], x_own[:, 0:1], XSCALE, ALU.mult, ALU.mult))

        def x_means_pe(pe):
            pe.wait_ge(x_dve, X_MEANS)
            nc.tensor.matmul(ps[:, SMALL, 0:8], cst["mean_all"], t8a[:, 0:8], start=True, stop=True).then_inc(x_pe, 1)

        def x_variances_pe(pe):
            pe.wait_ge(x_dve, X_MOMENTS)
            nc.tensor.matmul(ps[:, SMALL, 8:16], cst["mean_all"], t8b[:, 0:8], start=True, stop=True).then_inc(x_pe, 1)

        def x_roots_act(act):
            act.wait_ge(x_dve, X_VARIANCES)
            nc.scalar.activation(var8[:, 8:16], var8[:, 0:8], ACT.Sqrt).then_inc(x_act, 1)

        def load_natural(eng, src, i, arrived):
            for c in range(NC_):
                part = src[:, c * P:(c + 1) * P, 2 * BW * i:2 * BW * (i + 1), :].rearrange("b p w k -> p (b w k)")
                eng.dma_start(Zx[:, 8 * i:8 * (i + 1), c, :], part.rearrange("p (g n) -> p g n", g=8))\
                   .then_inc(arrived[i], 16)

        X_LOADED = 16 * NC_


        W_LARGEST = NG // 8 + 1

        with nc.Block() as block:
            @block.sync
            def _(sp):
                sp.dma_start(con[:, :], consts[:, :]).then_inc(const_in, 16)
                for i in range(NG // 8):
                    load_natural(sp, weight, i, w_in)

            @block.scalar
            def _(act):
                act.wait_ge(taps_zero, 1)
                for n in range(TW):
                    for dw in range(3):
                        at = (n - dw + 2) * C
                        act.dma_start(taps[n * C:(n + 1) * C, :, at:at + C],
                                      filters[:, dw, :, :].rearrange("h c o -> c h o")).then_inc(taps_in, 16)
                    act.dma_start(bias_p[n * C:(n + 1) * C, :], bias.rearrange("(c a) -> c a", a=1))\
                       .then_inc(bias_in, 16)
                act.wait_ge(bias_in, 16 * TW)

            @block.vector
            def _(dve):
                t = Tally(y_dve)
                nc.vector.memset(taps[:, :, :], 0.0).then_inc(taps_zero, 1)
                for i in range(NG // 8):
                    dve.wait_ge(w_in[i], X_LOADED)
                    t.done(nc.vector.tensor_reduce(w_max[:, i:i + 1],
                                                   Z[:, 8 * i:8 * i + 8, :].rearrange("p g w -> p (g w)"),
                                                   AX.X, ALU.max, apply_absolute_value=True))
                dve.wait_ge(t.sem, t.n)
                t.done(nc.vector.reduce_max(c1[3], w_max, AX.X))
                assert t.n == W_LARGEST
                dve.wait_ge(const_in, 16)
                largest_everywhere(dve, t, y_pe, 0)
                t.done(nc.vector.tensor_scalar(a_scale, c1[2], WTOP, None, ALU.mult))
                t.done(nc.vector.tensor_scalar(a_unscale, c1[1], 1.0 / (WTOP * XSCALE), None, ALU.mult))
                dve.wait_ge(t.sem, t.n)
                t.done(nc.vector.tensor_scalar(idct_s[:, :], cst["idct"], a_unscale, None, ALU.mult))
                dve.wait_ge(taps_in, 16 * 3 * TW)
                t.done(nc.vector.tensor_reduce(tap_max, taps[:, :, :].rearrange("p h w -> p (h w)"), AX.X, ALU.max,
                                               apply_absolute_value=True))

            @block.tensor
            def _(pe):
                pe.wait_ge(const_in, 16)
                pe.wait_ge(y_dve, W_LARGEST)
                largest_transpose(y_pe)
                pe.wait_ge(y_dve, W_LARGEST + 2)
                largest_broadcast(y_pe)
        end_block()

        def f_bank(g):
            return ps[:, AHEAD + g % 3, :]

        with nc.Block() as block:
            @block.sync
            def _(sp):
                for g in range(NG):
                    if g % 8 == 7:
                        sp.wait_ge(f_transposed, g + 1)
                        load_natural(sp, x[0:1], g // 8, x_in)
                    sp.wait_ge(f_lo, g + 1)
                    sp.dma_start(a_dram[:, TW * g:TW * (g + 1), :, :].rearrange("k n s o -> k n (s o)"),
                                 a_stage[:, g % STAGES, :, :].rearrange("p s o -> p (s o)"))\
                      .then_inc(stored[g % STAGES], 16)
                for r in range(STAGES):
                    sp.wait_ge(stored[r], 16 * (NG // STAGES))

            @block.tensor
            def _(pe):
                def transpose(g):
                    if g >= AHEAD:
                        pe.wait_ge(f_odd if g % 2 else f_even, (g - AHEAD) // 2 + 1)
                    for o in range(NC_):
                        last = nc.tensor.transpose(ps[:, g % AHEAD, o * P:(o + 1) * P], Zx[:, g, o, :], cst["ident"])
                    last.then_inc(f_transposed, 1)
                transpose(0)
                transpose(1)
                for g in range(NG):
                    if g + 2 < NG:
                        transpose(g + 2)
                    pe.wait_ge(f_odd if g % 2 else f_even, g // 2 + 1)
                    if g >= 3:
                        pe.wait_ge(f_lo, g - 2)
                    nc.tensor.matmul(f_bank(g), cst["dct"], xt[:, g % STAGES, :], start=True, stop=True)\
                      .then_inc(f_product, 1)
                x_means_pe(pe)
                x_variances_pe(pe)

            def wait_copy(eng, g):
                eng.wait_ge(f_transposed, g + 1)
                if g >= STAGES:
                    eng.wait_ge(f_product, g - STAGES + 1)

            @block.scalar
            def _(act):
                def copy(g):
                    wait_copy(act, g)
                    nc.scalar.activation(xt[:, g % STAGES, :], ps[:, g % AHEAD, :], ACT.Copy).then_inc(f_even, 1)
                copy(0)
                for g in range(NG):
                    if g % 2 == 0 and g + 2 < NG:
                        copy(g + 2)
                    act.wait_ge(f_product, g + 1)
                    if g >= STAGES:
                        act.wait_ge(stored[g % STAGES], 16 * (g // STAGES))
                    nc.scalar.activation(a_stage[:, g % STAGES, 0, :], f_bank(g), ACT.Copy, scale=a_scale)\
                      .then_inc(f_hi, 1)
                x_roots_act(act)

            @block.vector
            def _(dve):
                t = Tally(x_dve)

                def copy(g):
                    wait_copy(dve, g)
                    nc.vector.tensor_copy(xt[:, g % STAGES, :], ps[:, g % AHEAD, :]).then_inc(f_odd, 1)
                copy(1)
                for g in range(NG):
                    if g % 2 and g + 2 < NG:
                        copy(g + 2)
                    dve.wait_ge(f_hi, g + 1)
                    nc.vector.scalar_tensor_tensor(a_stage[:, g % STAGES, 1, :], f_bank(g), a_scale,
                                                   a_stage[:, g % STAGES, 0, :], ALU.mult, ALU.subtract)\
                      .then_inc(f_lo, 1)
                    if g % 8 == 7 and g >= 15:
                        x_stats_of(dve, t, g // 8 - 1)
                x_stats_of(dve, t, NG // 8 - 1)
                x_means(dve, t)
                x_moments(dve, t)
                x_scales(dve, t)
        end_block()


        def load_a(sp, k):
            sp.dma_start(a_ring[:, k % 2, :, :, :], a_dram[k, :, :, :].rearrange("(c p) s o -> p c s o", p=P))\
              .then_inc(a_in[k % 2], 16)

        def restage(sp, b, j):
            src = x[b, :, BW * j:BW * (j + 1), :].rearrange("b (c p) w k -> p (b c) (w k)", p=P)
            sp.dma_start(stage[:, j % 2, :, :], src).then_inc(restage_in[j % 2], 16)

        Y_MEAN = NG + 1
        Y_MOMENT, Y_VARIANCE = Y_MEAN + 4, Y_MEAN + 5
        Y_LARGEST = Y_VARIANCE + 5 + 7

        def regions():
            for j in range(NB + 1):
                w0, w1 = max(BW * j - REGION_LAG, 0), min(BW * (j + 1) - REGION_LAG, W)
                pieces = []
                for g in range(max(GB * j - 1, 0), min(GB * (j + 1), NG)):
                    first = TW * g - 1
                    a, z = max(first, w0), min(first + OW, w1)
                    pieces.append((g, (a - w0) * C, (a - first) * C, (z - first) * C))
                yield j, w0, w1, pieces

        NREG = NB + 1

        def image(b, following):
            with nc.Block() as block:
                @block.sync
                def _(sp):
                    load_a(sp, 0)
                    load_a(sp, 1)
                    restage(sp, b, 0)
                    restage(sp, b, 1)
                    for k in range(2, C):
                        sp.wait_ge(m_product, k - 1)
                        load_a(sp, k)
                    for j in range(2, NB):
                        sp.wait_ge(b_product, GB * (j - 1))
                        restage(sp, b, j)
                    for j, w0, w1, _ in regions():
                        if following is not None and j % 2 == 0 and j < NB:
                            sp.wait_ge(c_lo, GB * (j + 2))
                            load_natural(sp, x[following], j // 2, x_in)
                        for c in range(NC_):
                            n = NC_ * j + c
                            sp.wait_ge(c_out, n + 1)
                            dst = out[b, c * P:(c + 1) * P, w0:w1, :].rearrange("b p w k -> p (b w k)")
                            sp.dma_start(dst, out_stage[:, n % STAGES, 0:(w1 - w0) * C])\
                              .then_inc(stored[n % STAGES], 16)
                    for r in range(STAGES):
                        sp.wait_ge(stored[r], 16 * (NREG * NC_ // STAGES))

                def wait_slot(eng, g, transposed, product):
                    eng.wait_ge(transposed, g + 1)
                    if g >= STAGES:
                        eng.wait_ge(product, g - STAGES + 1)

                def f_out(g):
                    return ps[:, AHEAD + g % 4, :].rearrange("p (c k n) -> p (c k) n", c=NC_, k=C)

                def f_part(g, s):
                    return Z16[:, g, :, :, s, :].rearrange("p c k n -> p (c k) n")

                def m_copy(k, o):
                    src = ps[:, NC_ * (k % 2) + o:NC_ * (k % 2) + o + 2, :].rearrange("p o (g n) -> p o g n", n=TW)
                    z = Z[:, :, :].rearrange("p g (o k n) -> p o g k n", o=NC_, k=C)
                    return z[:, o:o + 2, :, k, :], src

                @block.tensor
                def _(pe):
                    def transpose(g, even, odd, done):
                        if g >= AHEAD:
                            pe.wait_ge(odd if g % 2 else even, (g - AHEAD) // 2 + 1)
                        for c in range(NC_):
                            last = nc.tensor.transpose(ps[:, g % AHEAD, c * P:(c + 1) * P], Zx[:, g, c, :],
                                                       cst["ident"])
                        last.then_inc(done, 1)

                    transpose(0, f_even, f_odd, f_transposed)
                    transpose(1, f_even, f_odd, f_transposed)
                    for g in range(NG):
                        if g + 2 < NG:
                            transpose(g + 2, f_even, f_odd, f_transposed)
                        pe.wait_ge(f_odd if g % 2 else f_even, g // 2 + 1)
                        if g >= 4:
                            pe.wait_ge(f_lo, g - 3)
                        for c in range(NC_):
                            last = nc.tensor.matmul(ps[:, AHEAD + g % 4, c * P:(c + 1) * P],
                                                    xt[:, g % STAGES, c * P:(c + 1) * P], dct_r[:, :],
                                                    start=True, stop=True)
                        last.then_inc(f_product, 1)

                    pe.wait_ge(f_lo, NG)
                    for k in range(C):
                        pe.wait_ge(a_in[k % 2], 16 * (k // 2 + 1))
                        if k >= 2:
                            pe.wait_ge(m_act, k - 1)
                            pe.wait_ge(m_dve, k - 1)
                        for o in range(NC_):
                            bank = ps[:, NC_ * (k % 2) + o, :].rearrange("p (g n) -> p g n", n=TW)
                            for c in range(NC_):
                                for w_part, x_part in ((0, 0), (0, 1), (1, 0)):
                                    last = nc.tensor.matmul(bank, a_ring[:, k % 2, c, w_part, o * P:(o + 1) * P],
                                                            Z16[:, :, c, k, x_part, :],
                                                            start=(c == 0 and w_part == 0 and x_part == 0),
                                                            stop=(c == NC_ - 1 and w_part == 1))
                        last.then_inc(m_product, 1)

                    pe.wait_ge(m_act, C)
                    pe.wait_ge(m_dve, C)
                    transpose(0, b_even, b_odd, b_transposed)
                    transpose(1, b_even, b_odd, b_transposed)
                    for g in range(NG):
                        if g + 2 < NG:
                            transpose(g + 2, b_even, b_odd, b_transposed)
                        j, i = divmod(g, GB)
                        bank = AHEAD + g % 4
                        pe.wait_ge(b_odd if g % 2 else b_even, g // 2 + 1)
                        if g >= 4:
                            pe.wait_ge(b_kept, g - 3)
                        nc.tensor.matmul(ps[:, bank, :], idct_s[:, :], xt[:, g % STAGES, :], start=True, stop=False,
                                         skip_group_check=True)
                        pe.wait_ge(restage_in[j % 2], 16 * (j // 2 + 1))
                        for c in range(NC_):
                            last = nc.tensor.matmul(ps[:, bank, c * P:(c + 1) * P],
                                                    stage[:, j % 2, c, i * P:(i + 1) * P], cst["ident"],
                                                    start=False, stop=(c == NC_ - 1), is_transpose=True,
                                                    skip_group_check=True)
                        last.then_inc(b_product, 1)

                    pe.wait_ge(y_dve, Y_MEAN)
                    nc.tensor.matmul(ps[:, SMALL, 0:1], cst["mean_group"], mv8[:, 0:1], start=True, stop=True)\
                      .then_inc(y_pe, 1)
                    pe.wait_ge(y_dve, Y_MOMENT)
                    nc.tensor.matmul(ps[:, SMALL, 1:2], cst["mean_group"], c1[7], start=True, stop=True)\
                      .then_inc(y_pe, 1)
                    pe.wait_ge(y_dve, Y_LARGEST)
                    nc.tensor.matmul(ps[:, SMALL, 272:272 + C], cst["eighth"], s16, start=True, stop=True)\
                      .then_inc(y_pe, 1)
                    largest_transpose(y_pe)
                    pe.wait_ge(y_dve, Y_LARGEST + 2)
                    largest_broadcast(y_pe)

                    pe.wait_ge(pads_zero, 2)
                    pe.wait_ge(y_act, 2)
                    pe.wait_ge(y_dve, Y_TAPS)
                    for j, _, _, pieces in regions():
                        pe.wait_ge(c_lo, min(GB * (j + 1), NG))
                        for c in range(NC_):
                            n = NC_ * j + c
                            if n >= CBANKS:
                                pe.wait_ge(c_out, n - CBANKS + 1)
                            for i, (g, at, lo, hi) in enumerate(pieces):
                                for dh in range(3):
                                    for s, t_part in ((0, taps_hi), (0, taps_lo), (1, taps_hi)):
                                        last = nc.tensor.matmul(
                                            ps[:, n % CBANKS, at:at + hi - lo],
                                            h_ring[:, g % HSLOTS, s, c * P + dh:c * P + dh + P], t_part[:, dh, lo:hi],
                                            start=(i == 0 and dh == 0 and s == 0 and t_part is taps_hi),
                                            stop=(i == len(pieces) - 1 and dh == 2 and s == 1),
                                            skip_group_check=True)
                            last.then_inc(c_product, 1)
                        if following is not None and j == NREG - 2:
                            x_means_pe(pe)
                    if following is not None:
                        x_variances_pe(pe)

                @block.scalar
                def _(act):
                    def centre(g):
                        wait_slot(act, g, f_transposed, f_product)
                        nc.scalar.activation(xt[:, g % STAGES, :], ps[:, g % AHEAD, :], ACT.Identity, bias=x_negmean)\
                          .then_inc(f_even, 1)
                    centre(0)
                    for g in range(NG):
                        if g % 2 == 0 and g + 2 < NG:
                            centre(g + 2)
                        act.wait_ge(f_product, g + 1)
                        nc.scalar.activation(f_part(g, 0), f_out(g), ACT.Copy).then_inc(f_hi, 1)

                    for k in range(C):
                        act.wait_ge(m_product, k + 1)
                        nc.scalar.activation(*m_copy(k, 0), ACT.Copy).then_inc(m_act, 1)

                    def copy(g):
                        wait_slot(act, g, b_transposed, b_product)
                        nc.scalar.activation(xt[:, g % STAGES, :], ps[:, g % AHEAD, :], ACT.Copy).then_inc(b_even, 1)
                    copy(0)
                    for g in range(NG):
                        if g % 2 == 0 and g + 2 < NG:
                            copy(g + 2)
                        act.wait_ge(b_product, g + 1)
                        nc.scalar.activation(Z[:, g, :], ps[:, AHEAD + g % 4, :], ACT.Copy).then_inc(b_kept, 1)
                    act.wait_ge(y_dve, Y_VARIANCE)
                    nc.scalar.activation(c1[12], c1[8], ACT.Sqrt).then_inc(y_act, 1)

                    def split(g):
                        if g >= HSLOTS:
                            act.wait_ge(c_product, NC_ * ((g - HSLOTS + 1) // GB + 1))
                        nc.scalar.activation(h_ring[:, g % HSLOTS, 0, 1:H + 1], Z[:, g, :], ACT.Identity,
                                             bias=h_shift, scale=h_scale).then_inc(c_hi, 1)
                        nc.scalar.activation(Z[:, g, :], Z[:, g, :], ACT.Identity,
                                             bias=h_shift, scale=h_scale).then_inc(c_norm, 1)
                    act.wait_ge(y_dve, Y_LARGEST)
                    for g in range(2):
                        split(g)
                    act.wait_ge(y_dve, Y_SCALED)
                    nc.scalar.activation(taps_hi[:, :, :], taps_s[:, :, :], ACT.Copy).then_inc(y_act, 1)
                    for g in range(2, NG):
                        split(g)
                    if following is not None:
                        x_roots_act(act)

                @block.vector
                def _(dve):
                    def centre(g):
                        wait_slot(dve, g, f_transposed, f_product)
                        nc.vector.tensor_scalar(xt[:, g % STAGES, :], ps[:, g % AHEAD, :], x_negmean, None, ALU.add)\
                          .then_inc(f_odd, 1)
                    centre(1)
                    for g in range(NG):
                        if g % 2 and g + 2 < NG:
                            centre(g + 2)
                        dve.wait_ge(f_hi, g + 1)
                        nc.vector.tensor_tensor(f_part(g, 1), f_out(g), f_part(g, 0), ALU.subtract).then_inc(f_lo, 1)

                    for k in range(C):
                        dve.wait_ge(m_product, k + 1)
                        nc.vector.tensor_copy(*m_copy(k, 2)).then_inc(m_dve, 1)

                    t = Tally(y_dve)

                    def copy(g):
                        wait_slot(dve, g, b_transposed, b_product)
                        nc.vector.tensor_copy(xt[:, g % STAGES, :], ps[:, g % AHEAD, :]).then_inc(b_odd, 1)

                    def stats(g):
                        dve.wait_ge(b_kept, g + 1)
                        t.done(nc.vector.bn_stats(ystat[:, g, :], Z[:, g, :]))
                    copy(1)
                    for g in range(NG):
                        if g % 2 and g + 2 < NG:
                            copy(g + 2)
                        if g >= 1:
                            stats(g - 1)
                    stats(NG - 1)
                    for edge in (0, H + 1):
                        nc.vector.memset(h_ring[:, :, :, edge:edge + 1], 0.0).then_inc(pads_zero, 1)

                    mean_p, var_p = mv8[:, 0:1], mv8[:, 1:2]
                    dve.wait_ge(t.sem, t.n)
                    t.done(nc.vector.bn_aggr(mv8[:, 0:2], ystat[:, :, :].rearrange("p g s -> p (g s)")))
                    assert t.n == Y_MEAN
                    dve.wait_ge(y_pe, 1)
                    t.done(nc.vector.tensor_copy(c1[4], ps[:, SMALL, 0:1]))
                    dve.wait_ge(t.sem, t.n)
                    t.done(nc.vector.tensor_tensor(c1[5], mean_p, c1[4], ALU.subtract))
                    dve.wait_ge(t.sem, t.n)
                    t.done(nc.vector.tensor_tensor(c1[6], c1[5], c1[5], ALU.mult))
                    dve.wait_ge(t.sem, t.n)
                    t.done(nc.vector.tensor_tensor(c1[7], c1[6], var_p, ALU.add))
                    assert t.n == Y_MOMENT
                    dve.wait_ge(y_pe, 2)
                    t.done(nc.vector.tensor_scalar(c1[8], ps[:, SMALL, 1:2], EPS, None, ALU.add))
                    assert t.n == Y_VARIANCE
                    dve.wait_ge(y_act, 1)
                    inverse_root(dve, t, c1[8], c1[9], c1[10], c1[11], c1[12])
                    t.done(nc.vector.tensor_tensor(c1[13], c1[8], c1[9], ALU.mult))
                    t.done(nc.vector.tensor_scalar(h_scale, c1[9], XSCALE, None, ALU.mult))
                    t.done(nc.vector.tensor_tensor(c1[14], c1[4], bias_p, ALU.add))
                    dve.wait_ge(t.sem, t.n)
                    t.done(nc.vector.tensor_tensor(c1[3], c1[13], tap_max, ALU.max))
                    t.done(nc.vector.tensor_scalar(h_shift, c1[4], h_scale, -1.0, ALU.mult, ALU.mult))
                    t.done(nc.vector.tensor_scalar(s16, cst["pick_channel"], c1[14], None, ALU.mult))
                    t.done(nc.vector.scalar_tensor_tensor(taps_s[:, 1, :], cst["centre"], c1[13], taps[:, 1, :],
                                                          ALU.mult, ALU.add))
                    assert t.n == Y_LARGEST
                    largest_everywhere(dve, t, y_pe, 3)
                    t.done(nc.vector.tensor_scalar(c1[15], c1[2], WTOP, None, ALU.mult))
                    t.done(nc.vector.tensor_scalar(conv_unscale, c1[1], 1.0 / (WTOP * XSCALE), None, ALU.mult))
                    t.done(nc.vector.tensor_copy(out_shift, ps[:, SMALL, 272:272 + C]))
                    dve.wait_ge(t.sem, t.n)
                    for h in (0, 2):
                        t.done(nc.vector.tensor_scalar(taps_s[:, h, :], taps[:, h, :], c1[15], None, ALU.mult))
                    t.done(nc.vector.tensor_scalar(taps_s[:, 1, :], taps_s[:, 1, :], c1[15], None, ALU.mult))
                    assert t.n == Y_SCALED
                    dve.wait_ge(y_act, 2)
                    t.done(nc.vector.tensor_tensor(taps_lo[:, :, :], taps_s[:, :, :], taps_hi[:, :, :], ALU.subtract))
                    assert t.n == Y_TAPS

                    tx = Tally(x_dve)
                    done = [0]

                    def split_to(upto):
                        for g in range(done[0], upto):
                            dve.wait_ge(c_norm, g + 1)
                            nc.vector.tensor_tensor(h_ring[:, g % HSLOTS, 1, 1:H + 1], Z[:, g, :],
                                                    h_ring[:, g % HSLOTS, 0, 1:H + 1], ALU.subtract).then_inc(c_lo, 1)
                        done[0] = max(done[0], upto)

                    for j, w0, w1, _ in regions():
                        split_to(min(GB * (j + 2), NG))
                        if following is not None and j >= 2:
                            if j % 2 == 0 and j < NB:
                                x_stats_of(dve, tx, j // 2 - 1)
                            if j == NB - 1:
                                x_stats_of(dve, tx, NG // 8 - 1)
                                x_means(dve, tx)
                            if j == NB:
                                x_moments(dve, tx)
                        for c in range(NC_):
                            n = NC_ * j + c
                            dve.wait_ge(c_product, n + 1)
                            if n >= STAGES:
                                dve.wait_ge(stored[n % STAGES], 16 * (n // STAGES))
                            w = w1 - w0
                            shift = out_shift.rearrange("p (a c) -> p a c", a=1).to_broadcast([P, w, C])
                            nc.vector.scalar_tensor_tensor(
                                out_stage[:, n % STAGES, 0:w * C].rearrange("p (w k) -> p w k", k=C),
                                ps[:, n % CBANKS, 0:w * C].rearrange("p (w k) -> p w k", k=C), conv_unscale, shift,
                                ALU.mult, ALU.add).then_inc(c_out, 1)
                    if following is not None:
                        x_scales(dve, tx)
            end_block()

        Y_SCALED = Y_LARGEST + 4 + 3 + 3
        Y_TAPS = Y_SCALED + 1

        with nc.Fori(0, B - 1) as b:
            image(bass.ds(b, 1), bass.ds(b + 1, 1))
        image(slice(B - 1, B), None)


_INS = ["x", "L0_conv_weight", "L1_conv_filters", "L1_conv_bias"]


def kernel(**inputs):
    import concourse.bacc as _bacc
    from concourse.bass_utils import run_bass_kernel_spmd as _run

    nc = _bacc.Bacc("TRN2", target_bir_lowering=False, num_devices=1)
    arrays, args = {}, []
    for name in _INS + ["consts"]:
        a = shape_constants() if name == "consts" else np.ascontiguousarray(inputs[name])
        if name == "L0_conv_weight":
            a = a[None]
        arrays[f"in_{name}"] = a
        args.append(nc.dram_tensor(f"in_{name}", a.shape, FP32, kind="ExternalInput").ap())
    out = nc.dram_tensor("out", (B, H, W, C), FP32, kind="ExternalOutput").ap()
    build(nc, *args, out)
    r = _run(nc, [arrays], core_ids=[0])
    return r.results[0]["out"]
```

```python
import numpy as np
import concourse.bass as bass
from concourse import mybir
from contextlib import ExitStack

FP32 = mybir.dt.float32
FP16 = mybir.dt.float16
I32 = mybir.dt.int32
ALU = mybir.AluOpType
ACT = mybir.ActivationFunctionType
AX = mybir.AxisListType

B, H, W, C = 8, 512, 512, 16
P = 128
TW = P // C
NG = W // TW
CHUNKS = H // P
TH = TW // 2
PAIRS = H // 2
HALVES = PAIRS // P
GROUPS, GC = 8, C // 8
EPS = 1e-5
GB = 4
NB = NG // GB
BW = GB * TW
RW = 16
BANK = 512
OW = TH + 2
TAPS = 4
AHEAD = 4
CBANKS = 7
SMALL = 7
STAGES = 4
XTS = 8
REGION_LAG = TH // 2
HSLOTS = 12
XSCALE = 16.0
WTOP = 256.0
EXPONENT_BITS = 0x7F800000
LEAST = 1e-30

CONST_COLS = {}
_at = 0
for _name, _n in (("ident", P), ("dct", P), ("idct", P), ("mean_all", P), ("mean_group", P), ("spread_group", P),
                  ("eighth", P), ("pick_group", GROUPS), ("pick_channel", C), ("centre", 2 * OW * C), ("ones", P)):
    CONST_COLS[_name] = (_at, _at + _n)
    _at += _n
CONST_N = _at


def shape_constants():
    k = np.arange(C)[:, None]
    n = np.arange(C)[None, :]
    m = np.sqrt(2.0 / C) * np.cos(np.pi * (2 * n + 1) * k / (2 * C))
    m[0, :] *= 1.0 / np.sqrt(2.0)
    p = np.arange(P)
    out = np.zeros((P, CONST_N), np.float32)

    def put(name, a):
        lo, hi = CONST_COLS[name]
        out[:, lo:hi] = a

    put("ident", np.eye(P))
    dct = np.zeros((TW, C, C, TW))
    for t in range(TW):
        dct[t, :, :, t] = m.T
    put("dct", dct.reshape(P, P))
    idct = np.zeros((2, C, TH, 2, TH, C))
    for r in range(2):
        for t in range(TH):
            idct[r, :, t, r, t, :] = m
    put("idct", idct.reshape(P, P))
    put("mean_all", np.full((P, P), 1.0 / P))
    same = ((p[:, None] % C) // GC == (p[None, :] % C) // GC)
    put("mean_group", same / (TW * GC))
    put("spread_group", np.full((P, P), 1.0 / (TW * GC)))
    put("eighth", np.full((P, P), 1.0 / TW))
    put("pick_group", (p[:, None] % C) // GC == np.arange(GROUPS)[None, :])
    put("pick_channel", (p[:, None] % C) == np.arange(C)[None, :])
    centre = np.zeros((P, 2, OW, C))
    centre[p, p // (TH * C), p // C % TH + 1, p % C] = 1.0
    put("centre", centre.reshape(P, 2 * OW * C))
    put("ones", np.ones((P, P)))
    return out


class Tally:

    def __init__(self, sem):
        self.sem, self.n = sem, 0

    def done(self, instruction):
        self.n += 1
        instruction.then_inc(self.sem, 1)
        return self.n


def build(nc, x, weight, filters, bias, consts, out):
    ctx = ExitStack()
    with ctx:
        def sb(name, shape, dt=FP32):
            return ctx.enter_context(nc.sbuf_tensor(name, shape, dt))

        a_dram = nc.dram_tensor("a_split", (C, H, 2, H), FP16, kind="Internal").ap()

        t_dram = nc.dram_tensor("x_transposed", (P, NG, 2, PAIRS), FP32, kind="Internal").ap()

        Z = sb("image", [P, NG, BANK])
        Zx = Z[:, :, :].rearrange("p g (c w) -> p g c w", c=CHUNKS)
        Z16 = Z[:, :, :].bitcast(FP16).rearrange("p g (c s k n) -> p g c s k n", c=CHUNKS, k=C, s=2)
        Zm = Z[:, :, :].rearrange("p g (h u r k n) -> p g h u r k n", h=HALVES, u=2, r=2, k=C)
        arena = sb("arena", [P, HSLOTS * 2 * 2 * (PAIRS + 2)], FP16)
        a_ring = arena[:, 0:2 * CHUNKS * 2 * H].rearrange("p (r c s o) -> p r c s o", r=2, c=CHUNKS, s=2)
        h_ring = arena[:, :].rearrange("p (r s u h) -> p r s u h", r=HSLOTS, s=2, u=2)
        stage = sb("stage", [P, 2, GB, BANK])
        out_stage = stage[:, :, :, :].rearrange("p a b w -> p (a b) w")
        a_stage = stage[:, :, :, :].rearrange("p a b w -> p (a b) w").bitcast(FP16).rearrange(
            "p r (s o) -> p r s o", s=2)
        xt = sb("transposed", [P, XTS, BANK])
        con = sb("constants", [P, CONST_N])
        cst = {n: con[:, lo:hi] for n, (lo, hi) in CONST_COLS.items()}
        dct_r = sb("dct_scaled", [P, P])
        idct_s = sb("idct_scaled", [P, P])
        taps = sb("taps", [P, TAPS, OW * C])
        taps_s = sb("taps_scaled", [P, TAPS, OW * C])
        taps_hi = sb("taps_hi", [P, TAPS, OW * C], FP16)
        taps_lo = sb("taps_lo", [P, TAPS, OW * C], FP16)
        xstat = sb("x_stats", [P, GROUPS, NG // 8, 6])
        ystat = sb("y_stats", [P, NG, 6])
        small = sb("small", [P, 512])
        ps = ctx.enter_context(nc.psum_tensor("banks", [P, SMALL + 1, BANK], FP32))

        def cols(n):
            at = small_at[0]
            small_at[0] += n
            return small[:, at:at + n]
        small_at = [0]

        a_scale, a_unscale, x_negmean, bias_p = (cols(1) for _ in range(4))
        h_scale, h_shift, conv_unscale, out_shift = cols(1), cols(1), cols(1), cols(C)
        w_max, row = cols(NG // 8), cols(P)
        own_largest, power, inverse_power, tap_power = (cols(1) for _ in range(4))
        x_mv = cols(2 * GROUPS).rearrange("p (q s) -> p q s", s=2)
        t8a, mean8, dev8, sq8, t8b, x_pick, x_pick2 = (cols(GROUPS) for _ in range(7))
        x_var, x_root, x_r, x_f = (cols(1) for _ in range(4))
        y_mv, y_var, y_root = cols(2), cols(1 + GROUPS), cols(1 + GROUPS)
        y_dev, y_moment, y_spread, y_mean, y_total = cols(1), cols(1), cols(GROUPS), cols(1), cols(1)
        y_channel, y_r, y_f, y_sd, y_largest = cols(C), cols(1), cols(1), cols(1), cols(1)

        sems = []

        def sem(name):
            s = ctx.enter_context(nc.semaphore(name))
            sems.append(s)
            return s

        const_in, taps_in, bias_in, taps_zero = sem("const_in"), sem("taps_in"), sem("bias_in"), sem("taps_zero")
        x_in = [sem(f"x_in{i}") for i in range(NG // 8)]
        w_in = [sem(f"w_in{i}") for i in range(NG // 8)]
        a_in = [sem(f"a_in{i}") for i in range(2)]
        restage_in = [sem(f"restage_in{i}") for i in range(2)]
        stored = [sem(f"stored{i}") for i in range(STAGES)]
        a_kept = [sem(f"a_kept{i}") for i in range(2 * GB)]
        xt_kept = [sem(f"xt_kept{i}") for i in range(XTS // 2)]
        f_transposed, f_copied, f_even, f_odd = (sem(n) for n in ("f_transposed", "f_copied", "f_even", "f_odd"))
        f_product, f_hi, f_lo = sem("f_product"), sem("f_hi"), sem("f_lo")
        m_product, m_act, m_dve = sem("m_product"), sem("m_act"), sem("m_dve")
        b_transposed, b_copied, b_product, b_sum = (sem(n) for n in ("b_transposed", "b_copied", "b_product", "b_sum"))
        pads_zero = sem("pads_zero")
        c_norm, c_lo, c_product, c_out = (sem(n) for n in ("c_norm", "c_lo", "c_product", "c_out"))
        x_dve, x_pe, x_act = sem("x_dve"), sem("x_pe"), sem("x_act")
        y_dve, y_pe, y_act = sem("y_dve"), sem("y_pe"), sem("y_act")
        nums = [s.num for s in sems]
        sem_range = range(min(nums), max(nums) + 1)
        assert len(sem_range) == len(sems)

        def end_block():
            nc.all_engine_barrier(sems_to_clear=sem_range)


        def largest_everywhere(dve, t, pe_sem, pe_before):
            dve.wait_ge(pe_sem, pe_before + 1)
            t.done(nc.vector.reduce_max(row[0:1, 0:1], ps[0:1, SMALL, 0:P], AX.X))
            dve.wait_ge(t.sem, t.n)
            t.done(nc.vector.tensor_scalar(row[0:1, 1:2], row[0:1, 0:1], LEAST, None, ALU.max))
            dve.wait_ge(pe_sem, pe_before + 2)
            t.done(nc.vector.tensor_scalar(power.bitcast(I32), ps[:, SMALL, 256:257].bitcast(I32), EXPONENT_BITS,
                                           None, ALU.bitwise_and))
            dve.wait_ge(t.sem, t.n)
            t.done(nc.vector.reciprocal(inverse_power, power))
            dve.wait_ge(t.sem, t.n)

        def largest_transpose(pe_sem):
            nc.tensor.transpose(ps[0:1, SMALL, 0:P], own_largest, cst["ident"]).then_inc(pe_sem, 1)

        def largest_broadcast(pe_sem):
            nc.tensor.matmul(ps[:, SMALL, 256:257], cst["ones"][0:1, :], row[0:1, 1:2], start=True, stop=True)\
              .then_inc(pe_sem, 1)

        VARIANCE_SCALE = 1.0 / (XSCALE * XSCALE)

        def newton(dve, t, v, root, r, f):
            t.done(nc.vector.reciprocal(r, root))
            dve.wait_ge(t.sem, t.n)
            t.done(nc.vector.scalar_tensor_tensor(f, r, r, v, ALU.mult, ALU.mult))
            dve.wait_ge(t.sem, t.n)
            t.done(nc.vector.tensor_scalar(f, f, -0.5, 1.5, ALU.mult, ALU.add))
            dve.wait_ge(t.sem, t.n)

        def x_stats_of(dve, t, i, groups=range(GROUPS)):
            dve.wait_ge(x_in[i], X_LOADED)
            v = Z[:, 8 * i:8 * i + 8, :].rearrange("p g w -> p (g w)").rearrange("p (n c) -> p n c", c=C)
            for q in groups:
                t.done(nc.vector.bn_stats(xstat[:, q, i, :], v[:, :, GC * q:GC * q + GC]))

        X_MEANS = GROUPS * (NG // 8) + GROUPS + 1
        X_MOMENTS, X_VARIANCES = X_MEANS + 3, X_MEANS + 9

        def x_means(dve, t):
            dve.wait_ge(t.sem, t.n)
            for q in range(GROUPS):
                t.done(nc.vector.bn_aggr(x_mv[:, q, :], xstat[:, q, :, :].rearrange("p j s -> p (j s)")))
            dve.wait_ge(t.sem, t.n)
            t.done(nc.vector.tensor_copy(t8a, x_mv[:, :, 0]))
            assert t.n == X_MEANS

        def x_moments(dve, t):
            dve.wait_ge(x_pe, 1)
            t.done(nc.vector.tensor_tensor(dev8, t8a, ps[:, SMALL, 0:8], ALU.subtract))
            dve.wait_ge(t.sem, t.n)
            t.done(nc.vector.tensor_tensor(sq8, dev8, dev8, ALU.mult))
            dve.wait_ge(t.sem, t.n)
            t.done(nc.vector.tensor_tensor(t8b, sq8, x_mv[:, :, 1], ALU.add))
            assert t.n == X_MOMENTS

        def x_scales(dve, t):
            t.done(nc.vector.tensor_tensor(mean8, t8a, dev8, ALU.subtract))
            dve.wait_ge(t.sem, t.n)
            t.done(nc.vector.tensor_tensor(x_pick, mean8, cst["pick_group"], ALU.mult))
            dve.wait_ge(t.sem, t.n)
            t.done(nc.vector.tensor_reduce(x_negmean, x_pick, AX.X, ALU.add, negate=True))
            dve.wait_ge(x_pe, 2)
            t.done(nc.vector.tensor_tensor(x_pick2, ps[:, SMALL, 8:16], cst["pick_group"], ALU.mult))
            dve.wait_ge(t.sem, t.n)
            t.done(nc.vector.reduce_sum(x_var, x_pick2, AX.X))
            dve.wait_ge(t.sem, t.n)
            t.done(nc.vector.tensor_scalar(x_var, x_var, EPS, VARIANCE_SCALE, ALU.add, ALU.mult))
            assert t.n == X_VARIANCES
            dve.wait_ge(x_act, 1)
            newton(dve, t, x_var, x_root, x_r, x_f)
            t.done(nc.vector.tensor_scalar(dct_r[:, :], cst["dct"], x_r, x_f, ALU.mult, ALU.mult))

        def x_means_pe(pe):
            pe.wait_ge(x_dve, X_MEANS)
            nc.tensor.matmul(ps[:, SMALL, 0:8], cst["mean_all"], t8a, start=True, stop=True).then_inc(x_pe, 1)

        def x_variances_pe(pe):
            pe.wait_ge(x_dve, X_MOMENTS)
            nc.tensor.matmul(ps[:, SMALL, 8:16], cst["mean_all"], t8b, start=True, stop=True).then_inc(x_pe, 1)

        def x_roots_act(act):
            act.wait_ge(x_dve, X_VARIANCES)
            nc.scalar.activation(x_root, x_var, ACT.Sqrt).then_inc(x_act, 1)

        def load_natural(eng, src, i, arrived):
            for c in range(CHUNKS):
                part = src[:, c * P:(c + 1) * P, 2 * BW * i:2 * BW * (i + 1), :].rearrange("b p w k -> p (b w k)")
                eng.dma_start(Zx[:, 8 * i:8 * (i + 1), c, :], part.rearrange("p (g n) -> p g n", g=8))\
                   .then_inc(arrived[i], 16)

        X_LOADED = 16 * CHUNKS


        W_LARGEST = NG // 8 + 1
        T_LARGEST = W_LARGEST + 8

        with nc.Block() as block:
            @block.sync
            def _(sp):
                sp.dma_start(con[:, :], consts[:, :]).then_inc(const_in, 16)
                for i in range(NG // 8):
                    load_natural(sp, weight, i, w_in)

            @block.scalar
            def _(act):
                act.wait_ge(taps_zero, 1)
                for q in range(TW):
                    r, n = divmod(q, TH)
                    sets = [(0, r + 1), (1, r), (2, 0) if r else (3, 2)]
                    for dw in range(3):
                        at = (n - dw + 2) * C
                        for t_set, dh in sets:
                            act.dma_start(taps[q * C:(q + 1) * C, t_set, at:at + C], filters[dh, dw, :, :])\
                               .then_inc(taps_in, 16)
                    act.dma_start(bias_p[q * C:(q + 1) * C, :], bias.rearrange("(c a) -> c a", a=1))\
                       .then_inc(bias_in, 16)
                act.wait_ge(bias_in, 16 * TW)

            @block.vector
            def _(dve):
                t = Tally(y_dve)
                nc.vector.memset(taps[:, :, :], 0.0).then_inc(taps_zero, 1)
                for i in range(NG // 8):
                    dve.wait_ge(w_in[i], X_LOADED)
                    t.done(nc.vector.tensor_reduce(w_max[:, i:i + 1],
                                                   Z[:, 8 * i:8 * i + 8, :].rearrange("p g w -> p (g w)"),
                                                   AX.X, ALU.max, apply_absolute_value=True))
                dve.wait_ge(t.sem, t.n)
                t.done(nc.vector.reduce_max(own_largest, w_max, AX.X))
                assert t.n == W_LARGEST
                dve.wait_ge(const_in, 16)
                largest_everywhere(dve, t, y_pe, 0)
                t.done(nc.vector.tensor_scalar(a_scale, inverse_power, WTOP, None, ALU.mult))
                t.done(nc.vector.tensor_scalar(a_unscale, power, 1.0 / (WTOP * XSCALE), None, ALU.mult))
                dve.wait_ge(t.sem, t.n)
                t.done(nc.vector.tensor_scalar(idct_s[:, :], cst["idct"], a_unscale, None, ALU.mult))
                dve.wait_ge(taps_in, 16 * 9 * TW)
                t.done(nc.vector.tensor_reduce(own_largest, taps[:, :, :].rearrange("p h w -> p (h w)"), AX.X, ALU.max,
                                               apply_absolute_value=True))
                assert t.n == T_LARGEST
                largest_everywhere(dve, t, y_pe, 2)
                t.done(nc.vector.tensor_copy(tap_power, power))

            @block.tensor
            def _(pe):
                pe.wait_ge(const_in, 16)
                pe.wait_ge(y_dve, W_LARGEST)
                largest_transpose(y_pe)
                pe.wait_ge(y_dve, W_LARGEST + 2)
                largest_broadcast(y_pe)
                pe.wait_ge(y_dve, T_LARGEST)
                largest_transpose(y_pe)
                pe.wait_ge(y_dve, T_LARGEST + 2)
                largest_broadcast(y_pe)
        end_block()

        AS = 2 * GB

        def f_bank(g):
            return ps[:, AHEAD + g % 3, :]

        with nc.Block() as block:
            @block.sync
            def _(sp):
                for g in range(NG):
                    if g % 8 == 7:
                        sp.wait_ge(f_transposed, g + 1)
                        load_natural(sp, x[0:1], g // 8, x_in)
                    sp.wait_ge(f_lo, g + 1)
                    sp.dma_start(a_dram[:, TW * g:TW * (g + 1), :, :].rearrange("k n s o -> k n (s o)"),
                                 a_stage[:, g % AS, :, :].rearrange("p s o -> p (s o)"))\
                      .then_inc(a_kept[g % AS], 16)
                for r in range(AS):
                    sp.wait_ge(a_kept[r], 16 * (NG // AS))

            @block.tensor
            def _(pe):
                def transpose(g):
                    if g >= AHEAD:
                        pe.wait_ge(f_copied, g - AHEAD + 1)
                    for o in range(CHUNKS):
                        last = nc.tensor.transpose(ps[:, g % AHEAD, o * P:(o + 1) * P], Zx[:, g, o, :], cst["ident"])
                    last.then_inc(f_transposed, 1)
                transpose(0)
                transpose(1)
                for g in range(NG):
                    if g + 2 < NG:
                        transpose(g + 2)
                    pe.wait_ge(f_copied, g + 1)
                    if g >= 3:
                        pe.wait_ge(f_lo, g - 2)
                    nc.tensor.matmul(f_bank(g), cst["dct"], xt[:, g % XTS, :], start=True, stop=True)\
                      .then_inc(f_product, 1)
                x_means_pe(pe)
                x_variances_pe(pe)

            def paired(a):
                return a.rearrange("p (h r i) -> p h i r", h=HALVES, r=2)

            def natural(a):
                return a.rearrange("p (h i r) -> p h i r", h=HALVES, r=2)

            @block.scalar
            def _(act):
                def copy(g):
                    act.wait_ge(f_transposed, g + 1)
                    if g >= XTS:
                        act.wait_ge(f_product, g - XTS + 1)
                    nc.scalar.activation(xt[:, g % XTS, :], ps[:, g % AHEAD, :], ACT.Copy).then_inc(f_copied, 1)
                copy(0)
                copy(1)
                for g in range(NG):
                    if g + 2 < NG:
                        copy(g + 2)
                    act.wait_ge(f_product, g + 1)
                    if g >= AS:
                        act.wait_ge(a_kept[g % AS], 16 * (g // AS))
                    nc.scalar.activation(paired(a_stage[:, g % AS, 0, :]), natural(f_bank(g)), ACT.Copy,
                                         scale=a_scale)\
                      .then_inc(f_hi, 1)
                x_roots_act(act)

            @block.vector
            def _(dve):
                t = Tally(x_dve)

                for g in range(NG):
                    dve.wait_ge(f_hi, g + 1)
                    low = None
                    for h in range(HALVES):
                        half = slice(h * 2 * P, (h + 1) * 2 * P)
                        low = nc.vector.scalar_tensor_tensor(
                            a_stage[:, g % AS, 1, half].rearrange("p (r i) -> p i r", r=2),
                            f_bank(g)[:, half].rearrange("p (i r) -> p i r", r=2), a_scale,
                            a_stage[:, g % AS, 0, half].rearrange("p (r i) -> p i r", r=2),
                            ALU.mult, ALU.subtract)
                    low.then_inc(f_lo, 1)
                    if g >= 12:
                        x_stats_of(dve, t, (g - 12) // 8, ((g - 12) % 8,))
                for n in range(NG - 12, NG):
                    x_stats_of(dve, t, n // 8, (n % 8,))
                x_means(dve, t)
                x_moments(dve, t)
                x_scales(dve, t)
        end_block()


        def load_a(sp, k):
            for h in range(HALVES):
                rows = a_dram[k, 2 * P * h:2 * P * (h + 1), :, :].rearrange("(i r) s o -> i r (s o)", r=2)
                sp.dma_start(a_ring[:, k % 2, 2 * h:2 * h + 2, :, :].rearrange("p c s o -> p c (s o)"), rows)\
                  .then_inc(a_in[k % 2], 16)

        A_LOADED = 16 * HALVES

        def keep(sp, m):
            i = 2 * m % XTS
            sp.dma_start(t_dram[:, 2 * m:2 * m + 2, :, :].rearrange("p g r i -> p (g r i)"),
                         xt[:, i:i + 2, :].rearrange("p g w -> p (g w)")).then_inc(xt_kept[m % (XTS // 2)], 16)

        def restage(sp, j):
            for r in range(2):
                for u in range(2):
                    sp.dma_start(stage[r * P // 2:(r + 1) * P // 2, j % 2, :, u * PAIRS:(u + 1) * PAIRS],
                                 t_dram[u * P // 2:(u + 1) * P // 2, GB * j:GB * (j + 1), r, :])\
                      .then_inc(restage_in[j % 2], 16)

        RESTAGED = 16 * 4

        Y_EARLY = 3 * NG // 4
        Y_MEAN = NG + 4 + 1
        Y_MOMENT, Y_VARIANCE = Y_MEAN + 3, Y_MEAN + 7
        Y_SHIFT = Y_VARIANCE + 5

        def regions():
            for j in range(NREG):
                w0, w1 = max(RW * j - REGION_LAG, 0), min(RW * (j + 1) - REGION_LAG, W)
                pieces = []
                per = RW // TH
                for t in range(max(per * j - 1, 0), min(per * (j + 1), 2 * NG)):
                    first = TH * t - 1
                    a, z = max(first, w0), min(first + OW, w1)
                    pieces.append((t // 2, t % 2, a - w0, a - first, z - first))
                yield j, w0, w1, pieces

        RG = RW // TW

        def split_goal(j):
            return min(RG * (j + 3) + min(j, 2 * RG), NG)

        LOAD_AT = {min(j for j in range(NG) if split_goal(j) >= 8 * (i + 1)): i for i in range(NG // 8)}
        NREG = W // RW + 1

        def image(b, following):
            with nc.Block() as block:
                @block.sync
                def _(sp):
                    load_a(sp, 0)
                    load_a(sp, 1)
                    for m in range(NG // 2):
                        sp.wait_ge(f_even, m + 1)
                        sp.wait_ge(f_odd, m + 1)
                        keep(sp, m)
                    for i in range(XTS // 2):
                        sp.wait_ge(xt_kept[i], 16 * (NG // XTS))
                    restage(sp, 0)
                    restage(sp, 1)
                    for k in range(2, C):
                        sp.wait_ge(m_product, k - 1)
                        load_a(sp, k)
                    for j in range(2, NB):
                        sp.wait_ge(b_sum, GB * (j - 1))
                        restage(sp, j)
                    for j, w0, w1, _ in regions():
                        if following is not None and j in LOAD_AT:
                            sp.wait_ge(c_lo, 8 * (LOAD_AT[j] + 1))
                            load_natural(sp, x[following], LOAD_AT[j], x_in)
                        for h in range(HALVES):
                            n = HALVES * j + h
                            sp.wait_ge(c_out, n + 1)
                            dst = out[b, 2 * P * h:2 * P * (h + 1), w0:w1, :]\
                                .rearrange("b (i r) w k -> i (b r) (w k)", r=2)
                            src = out_stage[:, n % STAGES, 0:2 * (w1 - w0) * C].rearrange("p (r w) -> p r w", r=2)
                            sp.dma_start(dst, src).then_inc(stored[n % STAGES], 16)
                    for r in range(STAGES):
                        sp.wait_ge(stored[r], 16 * len(range(r, HALVES * NREG, STAGES)))

                def wait_slot(eng, g, transposed, product):
                    eng.wait_ge(transposed, g + 1)
                    if g >= XTS:
                        eng.wait_ge(product, g - XTS + 1)

                def wait_kept(eng, g):
                    if g >= XTS:
                        eng.wait_ge(xt_kept[g // 2 % (XTS // 2)], 16 * (g // XTS))

                def f_in(g):
                    return ps[:, g % AHEAD, :].rearrange("p (i r) -> p r i", r=2)

                def f_centred(g):
                    return xt[:, g % XTS, :].rearrange("p (r i) -> p r i", r=2)

                def f_out(g):
                    return ps[:, AHEAD + g % 4, :].rearrange("p (c w) -> p c w", c=CHUNKS)

                def f_part(g, s):
                    return Z16[:, g, :, s, :, :].rearrange("p c k n -> p c (k n)")

                def m_copy(k, o):
                    src = ps[:, CHUNKS * (k % 2) + o, :].rearrange("p (g u n) -> p g u n", u=2, n=TH)
                    return Zm[:, :, o // 2, :, o % 2, k, :], src

                @block.tensor
                def _(pe):
                    def f_transpose(g):
                        if g >= AHEAD:
                            pe.wait_ge(f_odd if g % 2 else f_even, (g - AHEAD) // 2 + 1)
                        for c in range(CHUNKS):
                            last = nc.tensor.transpose(ps[:, g % AHEAD, c * P:(c + 1) * P], Zx[:, g, c, :],
                                                       cst["ident"])
                        last.then_inc(f_transposed, 1)

                    f_transpose(0)
                    f_transpose(1)
                    for g in range(NG):
                        if g + 2 < NG:
                            f_transpose(g + 2)
                        pe.wait_ge(f_odd if g % 2 else f_even, g // 2 + 1)
                        if g >= 4:
                            pe.wait_ge(f_lo, g - 3)
                        for c in range(CHUNKS):
                            h, r = divmod(c, 2)
                            rows = slice(r * PAIRS + h * P, r * PAIRS + (h + 1) * P)
                            last = nc.tensor.matmul(ps[:, AHEAD + g % 4, c * P:(c + 1) * P],
                                                    xt[:, g % XTS, rows], dct_r[:, :], start=True, stop=True)
                        last.then_inc(f_product, 1)

                    pe.wait_ge(f_lo, NG)
                    for k in range(C):
                        pe.wait_ge(a_in[k % 2], A_LOADED * (k // 2 + 1))
                        if k >= 2:
                            pe.wait_ge(m_act, k - 1)
                            pe.wait_ge(m_dve, k - 1)
                        for o in range(CHUNKS):
                            bank = ps[:, CHUNKS * (k % 2) + o, :].rearrange("p (g n) -> p g n", n=TW)
                            for c in range(CHUNKS):
                                for w_part, x_part in ((0, 0), (0, 1), (1, 0)):
                                    last = nc.tensor.matmul(bank, a_ring[:, k % 2, c, w_part, o * P:(o + 1) * P],
                                                            Z16[:, :, c, x_part, k, :],
                                                            start=(c == 0 and w_part == 0 and x_part == 0),
                                                            stop=(c == CHUNKS - 1 and w_part == 1))
                        last.then_inc(m_product, 1)

                    def b_transpose(g):
                        if g >= AHEAD:
                            pe.wait_ge(b_copied, g - AHEAD + 1)
                        for h in range(HALVES):
                            for u in range(2):
                                at = u * PAIRS + h * P
                                last = nc.tensor.transpose(ps[:, g % AHEAD, at:at + P], Zx[:, g, 2 * h + u, :],
                                                           cst["ident"])
                        last.then_inc(b_transposed, 1)

                    pe.wait_ge(m_act, C)
                    pe.wait_ge(m_dve, C)
                    b_transpose(0)
                    b_transpose(1)
                    for g in range(NG):
                        if g + 2 < NG:
                            b_transpose(g + 2)
                        pe.wait_ge(b_copied, g + 1)
                        if g >= 4:
                            pe.wait_ge(b_sum, g - 3)
                        nc.tensor.matmul(ps[:, AHEAD + g % 4, :], idct_s[:, :], xt[:, g % XTS, :],
                                         start=True, stop=True).then_inc(b_product, 1)

                    pe.wait_ge(y_dve, Y_MEAN)
                    nc.tensor.matmul(ps[:, SMALL, 0:1], cst["mean_group"], y_mv[:, 0:1], start=True, stop=True)\
                      .then_inc(y_pe, 1)
                    pe.wait_ge(y_dve, Y_MOMENT)
                    nc.tensor.matmul(ps[:, SMALL, 7:8], cst["mean_group"], y_moment, start=True, stop=True)
                    nc.tensor.matmul(ps[:, SMALL, 8:16], cst["spread_group"], y_spread, start=True, stop=True)\
                      .then_inc(y_pe, 1)
                    pe.wait_ge(y_dve, Y_SHIFT)
                    nc.tensor.matmul(ps[:, SMALL, 272:272 + C], cst["eighth"], y_channel, start=True, stop=True)\
                      .then_inc(y_pe, 1)

                    pe.wait_ge(pads_zero, 2)
                    pe.wait_ge(y_dve, Y_TAPS)
                    passes = ((0, taps_hi), (0, taps_lo), (1, taps_hi))
                    for j, w0, w1, pieces in regions():
                        if j > 0:
                            pe.wait_ge(c_lo, min(RG * (j + 1), NG))
                        for h in range(HALVES):
                            n = HALVES * j + h
                            if n >= CBANKS:
                                pe.wait_ge(c_out, n - CBANKS + 1)
                            w = w1 - w0
                            bank = ps[:, n % CBANKS, 0:2 * w * C].rearrange("p (r w) -> p r w", r=2)
                            for i, (g, u, at, lo, hi) in enumerate(pieces):
                                if n == 0:
                                    pe.wait_ge(c_lo, g + 1)
                                cols_out = slice(at * C, (at + hi - lo) * C)
                                for shift, rows, sets in ((0, slice(0, 2), slice(0, 2)), (-1, slice(0, 1), slice(2, 3)),
                                                          (1, slice(1, 2), slice(3, 4))):
                                    at_row = h * P + 1 + shift
                                    for s, t_part in passes:
                                        last = nc.tensor.matmul(
                                            bank[:, rows, cols_out],
                                            h_ring[:, g % HSLOTS, s, u, at_row:at_row + P],
                                            t_part[:, sets, lo * C:hi * C],
                                            start=(i == 0 and shift == 0 and s == 0 and t_part is taps_hi),
                                            stop=(i == len(pieces) - 1 and shift == 1 and s == 1),
                                            skip_group_check=True)
                            last.then_inc(c_product, 1)
                        if following is not None and j == NREG - 2:
                            x_means_pe(pe)
                    if following is not None:
                        x_variances_pe(pe)

                @block.scalar
                def _(act):
                    def centre(g):
                        wait_slot(act, g, f_transposed, f_product)
                        wait_kept(act, g)
                        nc.scalar.activation(f_centred(g), f_in(g), ACT.Identity, bias=x_negmean).then_inc(f_even, 1)
                    centre(0)
                    for g in range(NG):
                        if g % 2 == 0 and g + 2 < NG:
                            centre(g + 2)
                        act.wait_ge(f_product, g + 1)
                        nc.scalar.activation(f_part(g, 0), f_out(g), ACT.Copy).then_inc(f_hi, 1)

                    for k in range(C):
                        act.wait_ge(m_product, k + 1)
                        nc.scalar.activation(*m_copy(k, 0), ACT.Copy)
                        nc.scalar.activation(*m_copy(k, 1), ACT.Copy).then_inc(m_act, 1)

                    for i in range(XTS // 2):
                        act.wait_ge(xt_kept[i], 16 * (NG // XTS))
                    for g in range(NG):
                        wait_slot(act, g, b_transposed, b_product)
                        nc.scalar.activation(xt[:, g % XTS, :], ps[:, g % AHEAD, :], ACT.Copy).then_inc(b_copied, 1)
                    act.wait_ge(y_dve, Y_VARIANCE)
                    nc.scalar.activation(y_root, y_var, ACT.Sqrt).then_inc(y_act, 1)

                    def split(g):
                        if g >= HSLOTS:
                            act.wait_ge(c_product, HALVES * ((g - HSLOTS + 1) // RG + 1))
                        nc.scalar.activation(h_ring[:, g % HSLOTS, 0, :, 1:PAIRS + 1],
                                             Z[:, g, :].rearrange("p (u i) -> p u i", u=2), ACT.Identity,
                                             bias=h_shift, scale=h_scale)
                        nc.scalar.activation(Z[:, g, :], Z[:, g, :], ACT.Identity,
                                             bias=h_shift, scale=h_scale).then_inc(c_norm, 1)
                    act.wait_ge(y_dve, Y_SHIFT)
                    for g in range(NG):
                        split(g)
                    if following is not None:
                        x_roots_act(act)

                @block.vector
                def _(dve):
                    def centre(g):
                        wait_slot(dve, g, f_transposed, f_product)
                        wait_kept(dve, g)
                        nc.vector.tensor_scalar(f_centred(g), f_in(g), x_negmean, None, ALU.add).then_inc(f_odd, 1)
                    centre(1)
                    for g in range(NG):
                        if g % 2 and g + 2 < NG:
                            centre(g + 2)
                        dve.wait_ge(f_hi, g + 1)
                        nc.vector.tensor_tensor(f_part(g, 1), f_out(g), f_part(g, 0), ALU.subtract).then_inc(f_lo, 1)

                    for k in range(C):
                        dve.wait_ge(m_product, k + 1)
                        nc.vector.tensor_copy(*m_copy(k, 2))
                        nc.vector.tensor_copy(*m_copy(k, 3)).then_inc(m_dve, 1)

                    t = Tally(y_dve)

                    def stats(g):
                        dve.wait_ge(b_sum, g + 1)
                        t.done(nc.vector.bn_stats(ystat[:, g, :], Z[:, g, :]))

                    for g in range(NG):
                        j, i = divmod(g, GB)
                        dve.wait_ge(b_product, g + 1)
                        dve.wait_ge(restage_in[j % 2], RESTAGED * (j // 2 + 1))
                        nc.vector.tensor_tensor(Z[:, g, :], ps[:, AHEAD + g % 4, :], stage[:, j % 2, i, :], ALU.add)\
                          .then_inc(b_sum, 1)
                        if g >= 1:
                            stats(g - 1)
                        if g == Y_EARLY + 1:
                            early = ystat[:, 0:Y_EARLY, :].rearrange("p g s -> p (g s)")
                            dve.wait_ge(t.sem, t.n)
                            t.done(nc.vector.bn_aggr(y_mv, early))
                            dve.wait_ge(t.sem, t.n)
                            t.done(nc.vector.memset(ystat[:, Y_EARLY - 1, 3:4], float(Y_EARLY * BANK)))
                            t.done(nc.vector.tensor_copy(ystat[:, Y_EARLY - 1, 4:5], y_mv[:, 0:1]))
                            t.done(nc.vector.tensor_scalar(ystat[:, Y_EARLY - 1, 5:6], y_mv[:, 1:2],
                                                           float(Y_EARLY * BANK), None, ALU.mult))
                    stats(NG - 1)
                    for edge in (0, PAIRS + 1):
                        nc.vector.memset(h_ring[:, :, :, :, edge:edge + 1].rearrange("p r s u h -> p (r s u) h"), 0.0)\
                          .then_inc(pads_zero, 1)

                    mean_p, var_p = y_mv[:, 0:1], y_mv[:, 1:2]
                    dve.wait_ge(t.sem, t.n)
                    t.done(nc.vector.bn_aggr(y_mv, ystat[:, :, :].rearrange("p g s -> p (g s)")[:, 6 * Y_EARLY - 3:]))
                    assert t.n == Y_MEAN
                    dve.wait_ge(y_pe, 1)
                    t.done(nc.vector.tensor_tensor(y_dev, mean_p, ps[:, SMALL, 0:1], ALU.subtract))
                    dve.wait_ge(t.sem, t.n)
                    t.done(nc.vector.scalar_tensor_tensor(y_moment, y_dev, y_dev, var_p, ALU.mult, ALU.add))
                    dve.wait_ge(t.sem, t.n)
                    t.done(nc.vector.tensor_scalar(y_spread, cst["pick_group"], y_moment, None, ALU.mult))
                    assert t.n == Y_MOMENT
                    t.done(nc.vector.tensor_tensor(y_mean, mean_p, y_dev, ALU.subtract))
                    dve.wait_ge(t.sem, t.n)
                    t.done(nc.vector.scalar_tensor_tensor(y_total, y_mean, x_negmean, bias_p, ALU.subtract, ALU.add))
                    dve.wait_ge(t.sem, t.n)
                    t.done(nc.vector.tensor_scalar(y_channel, cst["pick_channel"], y_total, None, ALU.mult))
                    dve.wait_ge(y_pe, 2)
                    t.done(nc.vector.tensor_scalar(y_var, ps[:, SMALL, 7:8 + GROUPS], EPS, VARIANCE_SCALE, ALU.add,
                                                   ALU.mult))
                    assert t.n == Y_VARIANCE
                    dve.wait_ge(y_act, 1)
                    newton(dve, t, y_var[:, 0:1], y_root[:, 0:1], y_r, y_f)
                    t.done(nc.vector.tensor_scalar(h_scale, y_r, y_f, None, ALU.mult))
                    dve.wait_ge(t.sem, t.n)
                    t.done(nc.vector.tensor_scalar(h_shift, y_mean, h_scale, -1.0, ALU.mult, ALU.mult))
                    assert t.n == Y_SHIFT
                    t.done(nc.vector.tensor_scalar(y_sd, y_var[:, 0:1], h_scale, XSCALE, ALU.mult, ALU.mult))
                    t.done(nc.vector.reduce_max(y_largest, y_root[:, 1:], AX.X))
                    dve.wait_ge(t.sem, t.n)
                    t.done(nc.vector.scalar_tensor_tensor(taps_s[:, 0:2, :].rearrange("p t w -> p (t w)"),
                                                          cst["centre"], y_sd,
                                                          taps[:, 0:2, :].rearrange("p t w -> p (t w)"),
                                                          ALU.mult, ALU.add))
                    t.done(nc.vector.tensor_scalar(own_largest, y_largest, XSCALE, tap_power, ALU.mult, ALU.max))
                    dve.wait_ge(t.sem, t.n)
                    t.done(nc.vector.tensor_scalar(power.bitcast(I32), own_largest.bitcast(I32), EXPONENT_BITS, None,
                                                   ALU.bitwise_and))
                    dve.wait_ge(t.sem, t.n)
                    t.done(nc.vector.reciprocal(inverse_power, power))
                    t.done(nc.vector.tensor_scalar(conv_unscale, power, 1.0 / (WTOP * XSCALE), None, ALU.mult))
                    dve.wait_ge(t.sem, t.n)
                    for of, sets in ((taps_s, slice(0, 2)), (taps, slice(2, 4))):
                        t.done(nc.vector.tensor_scalar(taps_s[:, sets, :], of[:, sets, :], inverse_power, WTOP,
                                                       ALU.mult, ALU.mult))
                    assert t.n == Y_SCALED
                    dve.wait_ge(t.sem, t.n)
                    t.done(nc.vector.tensor_copy(taps_hi[:, :, :], taps_s[:, :, :]))
                    dve.wait_ge(t.sem, t.n)
                    t.done(nc.vector.tensor_tensor(taps_lo[:, :, :], taps_s[:, :, :], taps_hi[:, :, :], ALU.subtract))
                    assert t.n == Y_TAPS
                    dve.wait_ge(y_pe, 3)
                    t.done(nc.vector.tensor_copy(out_shift, ps[:, SMALL, 272:272 + C]))

                    tx = Tally(x_dve)
                    done = [0]

                    def split_to(upto):
                        for g in range(done[0], upto):
                            dve.wait_ge(c_norm, g + 1)
                            nc.vector.tensor_tensor(h_ring[:, g % HSLOTS, 1, :, 1:PAIRS + 1],
                                                    Z[:, g, :].rearrange("p (u i) -> p u i", u=2),
                                                    h_ring[:, g % HSLOTS, 0, :, 1:PAIRS + 1], ALU.subtract)\
                              .then_inc(c_lo, 1)
                        done[0] = max(done[0], upto)

                    for j, w0, w1, _ in regions():
                        split_to(split_goal(j))
                        if following is not None:
                            for back, groups in ((3, (0, 1)), (4, (2, 3)), (5, (4, 5)), (6, (6, 7))):
                                i = LOAD_AT.get(j - back)
                                if i is not None and i < NG // 8 - 1:
                                    x_stats_of(dve, tx, i, groups)
                            if j == NREG - 4:
                                x_stats_of(dve, tx, NG // 8 - 1, range(0, 4))
                            if j == NREG - 3:
                                x_stats_of(dve, tx, NG // 8 - 1, range(4, 8))
                                x_means(dve, tx)
                            if j == NREG - 1:
                                x_moments(dve, tx)
                        for h in range(HALVES):
                            n = HALVES * j + h
                            dve.wait_ge(c_product, n + 1)
                            if n >= STAGES:
                                dve.wait_ge(stored[n % STAGES], 16 * (n // STAGES))
                            w = 2 * (w1 - w0)
                            shift = out_shift.rearrange("p (a c) -> p a c", a=1).to_broadcast([P, w, C])
                            nc.vector.scalar_tensor_tensor(
                                out_stage[:, n % STAGES, 0:w * C].rearrange("p (w k) -> p w k", k=C),
                                ps[:, n % CBANKS, 0:w * C].rearrange("p (w k) -> p w k", k=C), conv_unscale, shift,
                                ALU.mult, ALU.add).then_inc(c_out, 1)
                    if following is not None:
                        x_scales(dve, tx)
            end_block()

        Y_SCALED = Y_SHIFT + 9
        Y_TAPS = Y_SCALED + 2

        with nc.Fori(0, B - 1) as b:
            image(bass.ds(b, 1), bass.ds(b + 1, 1))
        image(slice(B - 1, B), None)


_INS = ["x", "L0_conv_weight", "L1_conv_filters", "L1_conv_bias"]


def kernel(**inputs):
    import concourse.bacc as _bacc
    from concourse.bass_utils import run_bass_kernel_spmd as _run

    nc = _bacc.Bacc("TRN2", target_bir_lowering=False, num_devices=1)
    arrays, args = {}, []
    for name in _INS + ["consts"]:
        a = shape_constants() if name == "consts" else np.ascontiguousarray(inputs[name])
        if name == "L0_conv_weight":
            a = a[None]
        arrays[f"in_{name}"] = a
        args.append(nc.dram_tensor(f"in_{name}", a.shape, FP32, kind="ExternalInput").ap())
    out = nc.dram_tensor("out", (B, H, W, C), FP32, kind="ExternalOutput").ap()
    build(nc, *args, out)
    r = _run(nc, [arrays], core_ids=[0])
    return r.results[0]["out"]
```
